# Optimizing a Trainium2 kernel written in Bass

```python
import numpy as np
import jax
import jax.numpy as jnp

def _softmax(x, axis=-1):
    return jax.nn.softmax(x, axis=axis)

def _gelu(x):
    return jax.nn.gelu(x, approximate=True)

def _silu(x):
    return jax.nn.silu(x)

def _sigmoid(x):
    return jax.nn.sigmoid(x)

def _layernorm(x, axis=-1, eps=1e-05):
    m = jnp.mean(x, axis=axis, keepdims=True)
    v = jnp.var(x, axis=axis, keepdims=True)
    return (x - m) / jnp.sqrt(v + eps)

def _scatter_add(tgt, idx, src, axis=0):
    return tgt.at[idx].add(src)

def _segment_sum(src, seg, n):
    return jax.ops.segment_sum(src, seg, n)
kernel_name = 'mk_dlrm_tower_d1_rec_r8_00488c'

def setup_inputs(seed: int=0):
    np.random.seed(seed)
    _w = jnp.asarray

    def _rec_inputs():
        import jax
        import jax.numpy as jnp
        _tk = jax.random.key(seed)
        ids = jnp.stack([jax.random.randint(jax.random.fold_in(_tk, 200 + f), (2048,), 0, v, jnp.int32) for f, v in enumerate([12500, 1000, 12500, 1000, 125000, 1000, 1000, 1000, 1000, 1000, 12500, 1000, 12500, 1000, 12500, 1250, 1250, 12500, 1250, 1000, 12500, 1000, 12500, 1250, 12500, 1000])], axis=1)
        tbl_0 = 0.05 * jax.random.normal(jax.random.fold_in(_tk, 500 + 0), (12500, 128), jnp.float32)
        tbl_1 = 0.05 * jax.random.normal(jax.random.fold_in(_tk, 500 + 1), (1000, 128), jnp.float32)
        tbl_2 = 0.05 * jax.random.normal(jax.random.fold_in(_tk, 500 + 2), (12500, 128), jnp.float32)
        tbl_3 = 0.05 * jax.random.normal(jax.random.fold_in(_tk, 500 + 3), (1000, 128), jnp.float32)
        tbl_4 = 0.05 * jax.random.normal(jax.random.fold_in(_tk, 500 + 4), (125000, 128), jnp.float32)
        tbl_5 = 0.05 * jax.random.normal(jax.random.fold_in(_tk, 500 + 5), (1000, 128), jnp.float32)
        tbl_6 = 0.05 * jax.random.normal(jax.random.fold_in(_tk, 500 + 6), (1000, 128), jnp.float32)
        tbl_7 = 0.05 * jax.random.normal(jax.random.fold_in(_tk, 500 + 7), (1000, 128), jnp.float32)
        tbl_8 = 0.05 * jax.random.normal(jax.random.fold_in(_tk, 500 + 8), (1000, 128), jnp.float32)
        tbl_9 = 0.05 * jax.random.normal(jax.random.fold_in(_tk, 500 + 9), (1000, 128), jnp.float32)
        tbl_10 = 0.05 * jax.random.normal(jax.random.fold_in(_tk, 500 + 10), (12500, 128), jnp.float32)
        tbl_11 = 0.05 * jax.random.normal(jax.random.fold_in(_tk, 500 + 11), (1000, 128), jnp.float32)
        tbl_12 = 0.05 * jax.random.normal(jax.random.fold_in(_tk, 500 + 12), (12500, 128), jnp.float32)
        tbl_13 = 0.05 * jax.random.normal(jax.random.fold_in(_tk, 500 + 13), (1000, 128), jnp.float32)
        tbl_14 = 0.05 * jax.random.normal(jax.random.fold_in(_tk, 500 + 14), (12500, 128), jnp.float32)
        tbl_15 = 0.05 * jax.random.normal(jax.random.fold_in(_tk, 500 + 15), (1250, 128), jnp.float32)
        tbl_16 = 0.05 * jax.random.normal(jax.random.fold_in(_tk, 500 + 16), (1250, 128), jnp.float32)
        tbl_17 = 0.05 * jax.random.normal(jax.random.fold_in(_tk, 500 + 17), (12500, 128), jnp.float32)
        tbl_18 = 0.05 * jax.random.normal(jax.random.fold_in(_tk, 500 + 18), (1250, 128), jnp.float32)
        tbl_19 = 0.05 * jax.random.normal(jax.random.fold_in(_tk, 500 + 19), (1000, 128), jnp.float32)
        tbl_20 = 0.05 * jax.random.normal(jax.random.fold_in(_tk, 500 + 20), (12500, 128), jnp.float32)
        tbl_21 = 0.05 * jax.random.normal(jax.random.fold_in(_tk, 500 + 21), (1000, 128), jnp.float32)
        tbl_22 = 0.05 * jax.random.normal(jax.random.fold_in(_tk, 500 + 22), (12500, 128), jnp.float32)
        tbl_23 = 0.05 * jax.random.normal(jax.random.fold_in(_tk, 500 + 23), (1250, 128), jnp.float32)
        tbl_24 = 0.05 * jax.random.normal(jax.random.fold_in(_tk, 500 + 24), (12500, 128), jnp.float32)
        tbl_25 = 0.05 * jax.random.normal(jax.random.fold_in(_tk, 500 + 25), (1000, 128), jnp.float32)
        _rk = jax.random.fold_in(_tk, 7)
        r_dense_features = -0.000520686 + 1.00062 * jax.random.normal(jax.random.fold_in(_rk, 101), (2048, 128), jnp.float32)
        W_top1 = 0.0405887 * jax.random.normal(jax.random.fold_in(_tk, 801), (607, 512), jnp.float32)
        W_top2 = 0.0441942 * jax.random.normal(jax.random.fold_in(_tk, 802), (512, 256), jnp.float32)
        W_top3 = 0.0625 * jax.random.normal(jax.random.fold_in(_tk, 803), (256, 1), jnp.float32)
        b_top1 = jnp.zeros((512,), jnp.float32)
        b_top2 = jnp.zeros((256,), jnp.float32)
        return (r_dense_features, ids, tbl_0, tbl_1, tbl_2, tbl_3, tbl_4, tbl_5, tbl_6, tbl_7, tbl_8, tbl_9, tbl_10, tbl_11, tbl_12, tbl_13, tbl_14, tbl_15, tbl_16, tbl_17, tbl_18, tbl_19, tbl_20, tbl_21, tbl_22, tbl_23, tbl_24, tbl_25, W_top1, b_top1, W_top2, b_top2, W_top3)
    r_dense_features, ids, tbl_0, tbl_1, tbl_2, tbl_3, tbl_4, tbl_5, tbl_6, tbl_7, tbl_8, tbl_9, tbl_10, tbl_11, tbl_12, tbl_13, tbl_14, tbl_15, tbl_16, tbl_17, tbl_18, tbl_19, tbl_20, tbl_21, tbl_22, tbl_23, tbl_24, tbl_25, W_top1, b_top1, W_top2, b_top2, W_top3 = _rec_inputs()

    def _L0_rec_setup():
        import jax, jax.numpy as jnp
        import numpy as np
        NUM_SPARSE = 26
        EMBED_DIM = 128
        BATCH = 2048
        key = jax.random.key(seed)
        k1, k2 = jax.random.split(key)
        dense_features = jax.random.normal(k1, (BATCH, EMBED_DIM), dtype=jnp.float32)
        sparse_features = jax.random.normal(k2, (BATCH, NUM_SPARSE, EMBED_DIM), dtype=jnp.float32)
        return {'dense_features': dense_features, 'sparse_features': sparse_features}
    _L0_rec_all = _L0_rec_setup()
    _L0_rec_in = {k: v for k, v in _L0_rec_all.items() if k in ()}
    del _L0_rec_all
    return {'r_dense_features': r_dense_features, 'ids': ids, 'tbl_0': tbl_0, 'tbl_1': tbl_1, 'tbl_2': tbl_2, 'tbl_3': tbl_3, 'tbl_4': tbl_4, 'tbl_5': tbl_5, 'tbl_6': tbl_6, 'tbl_7': tbl_7, 'tbl_8': tbl_8, 'tbl_9': tbl_9, 'tbl_10': tbl_10, 'tbl_11': tbl_11, 'tbl_12': tbl_12, 'tbl_13': tbl_13, 'tbl_14': tbl_14, 'tbl_15': tbl_15, 'tbl_16': tbl_16, 'tbl_17': tbl_17, 'tbl_18': tbl_18, 'tbl_19': tbl_19, 'tbl_20': tbl_20, 'tbl_21': tbl_21, 'tbl_22': tbl_22, 'tbl_23': tbl_23, 'tbl_24': tbl_24, 'tbl_25': tbl_25, 'W_top1': W_top1, 'b_top1': b_top1, 'W_top2': W_top2, 'b_top2': b_top2, 'W_top3': W_top3}

def reference(r_dense_features, ids, tbl_0, tbl_1, tbl_2, tbl_3, tbl_4, tbl_5, tbl_6, tbl_7, tbl_8, tbl_9, tbl_10, tbl_11, tbl_12, tbl_13, tbl_14, tbl_15, tbl_16, tbl_17, tbl_18, tbl_19, tbl_20, tbl_21, tbl_22, tbl_23, tbl_24, tbl_25, W_top1, b_top1, W_top2, b_top2, W_top3):
    import jax
    import jax.numpy as jnp

    def _L0_rec_ref(dense_features, sparse_features):
        import jax, jax.numpy as jnp
        import numpy as np
        NUM_SPARSE = 26
        EMBED_DIM = 128
        BATCH = 2048
        F = NUM_SPARSE + 1
        combined = jnp.concatenate([dense_features[:, None, :], sparse_features], axis=1)
        interactions = jnp.einsum('bfd,bgd->bfg', combined, combined)
        iu, ju = jnp.triu_indices(F, k=1)
        interactions_flat = interactions[:, iu, ju]
        return jnp.concatenate([dense_features, interactions_flat], axis=1)
    e = jnp.stack([tbl_0[ids[:, 0]], tbl_1[ids[:, 1]], tbl_2[ids[:, 2]], tbl_3[ids[:, 3]], tbl_4[ids[:, 4]], tbl_5[ids[:, 5]], tbl_6[ids[:, 6]], tbl_7[ids[:, 7]], tbl_8[ids[:, 8]], tbl_9[ids[:, 9]], tbl_10[ids[:, 10]], tbl_11[ids[:, 11]], tbl_12[ids[:, 12]], tbl_13[ids[:, 13]], tbl_14[ids[:, 14]], tbl_15[ids[:, 15]], tbl_16[ids[:, 16]], tbl_17[ids[:, 17]], tbl_18[ids[:, 18]], tbl_19[ids[:, 19]], tbl_20[ids[:, 20]], tbl_21[ids[:, 21]], tbl_22[ids[:, 22]], tbl_23[ids[:, 23]], tbl_24[ids[:, 24]], tbl_25[ids[:, 25]]], axis=1)
    z = _L0_rec_ref(r_dense_features, e)
    z = z.reshape(z.shape[0], -1)
    h = jnp.concatenate([z, r_dense_features], axis=1)
    h = jnp.maximum(h @ W_top1 + b_top1, 0.0)
    h = jnp.maximum(h @ W_top2 + b_top2, 0.0)
    y = h @ W_top3
    return y

_drawn_inputs = setup_inputs


def setup_inputs(seed=0):
    import zlib

    import numpy as np

    out = dict(_drawn_inputs(seed))
    spreads = {'b_top1': (0.0, 0.1), 'b_top2': (0.0, 0.1)}
    factors = {}
    for name, (base, spread) in spreads.items():
        noise = np.random.default_rng([zlib.crc32(name.encode()), seed]).standard_normal(out[name].shape)
        drawn = base * np.exp(spread * noise) if base else spread * noise
        out[name] = jnp.asarray(drawn.astype(out[name].dtype))
    for name, factor in factors.items():
        out[name] = (out[name] * factor).astype(out[name].dtype)
    return out
```

```python
from contextlib import ExitStack

import concourse.bass as bass
from concourse import mybir

F32 = mybir.dt.float32
I32 = mybir.dt.int32
ALU = mybir.AluOpType
ACT = mybir.ActivationFunctionType

P = 128
QUAD = 32
PER = P // QUAD
TILES = 4
BANK = 512


def dlrm_kernel(nc: bass.Bass, dense, ids, tables, W1, b1, W2, b2, W3, out):
    B, D = dense.shape
    NT = len(tables)
    F = NT + 1
    H1, H2 = W1.shape[1], W2.shape[1]
    PAIRS = F * (F - 1) // 2
    MACRO = TILES * P
    NM = B // MACRO
    KC = next(k for k in range(1, 9) if PAIRS % k == 0 and PAIRS // k <= P)
    KP = PAIRS // KC
    N1, N2 = H1 // P, H2 // P
    GROUPS = MACRO // PER
    assert D == P and GROUPS == P and MACRO == BANK and F <= QUAD
    first_pair = [f * F - f * (f + 1) // 2 for f in range(F)]

    feature_groups = [list(range(f, min(f + 4, F))) for f in range(0, F, 4)]
    NG = len(feature_groups)
    UNIT_BANKS = 2
    PER_BANK = 4
    UNIT = UNIT_BANKS * PER_BANK
    UNITS = P // PER // UNIT
    SW = PER * F

    ZP = list(range(0, F - 1, 4))
    n_tail = len(ZP) + KC + N1 + N2 + 1
    Q_CHUNK, Q_H1, Q_H2, Q_Y = len(ZP), len(ZP) + KC, len(ZP) + KC + N1, n_tail - 1
    uses = [(n_tail + 1) // 2, n_tail // 2]

    with ExitStack() as ctx:
        def sb(name, shape, dt=F32):
            return ctx.enter_context(nc.sbuf_tensor(name, shape, dt))

        def ps(name, shape):
            return ctx.enter_context(nc.psum_tensor(name, shape, F32))

        def sem(name):
            return ctx.enter_context(nc.semaphore(name))

        ident = sb("ident", [P, P])
        ids_sb = sb("ids_sb", [P, B // P, NT], I32)
        idx = [sb(f"idx{p}", [P, NT], I32) for p in range(2)]
        rows = [sb(f"rows{p}", [P, F, D]) for p in range(2)]
        x = [sb(f"x{p}", [D, P, QUAD]) for p in range(2)]
        dense_t = sb("dense_t", [D, PER, GROUPS])
        gram = sb("gram", [P, GROUPS, F])
        pairs = sb("pairs", [GROUPS, PER, PAIRS])
        pairs_t = sb("pairs_t", [KP, KC, MACRO])
        w1a = sb("w1a", [P, H1])
        w1b = sb("w1b", [P, H1])
        w1d = sb("w1d", [P, H1])
        w1p = sb("w1p", [KP, KC, H1])
        w2 = sb("w2", [P, N1, H2])
        w3 = sb("w3", [P, N2])
        bias1 = sb("bias1", [P, N1])
        bias2 = sb("bias2", [P, N2])
        h1 = sb("h1", [P, N1, MACRO])
        h2 = sb("h2", [P, N2, MACRO])
        y = sb("y", [GROUPS, NM, PER])

        x_ps = [ps(f"x_ps{i}", [P, 4, P]) for i in range(2)]
        gram_ps = [ps(f"gram_ps{i}", [P, UNIT_BANKS, BANK]) for i in range(2)]
        tail_ps = [ps(f"tail_ps{i}", [P, BANK]) for i in range(2)]

        ids_loaded = sem("ids_loaded")
        dense_loaded = [sem(f"dense_loaded{p}") for p in range(2)]
        weights_loaded = sem("weights_loaded")
        ident_ready = sem("ident_ready")
        pads_ready = sem("pads_ready")
        dense_w_ready = sem("dense_w_ready")
        idx_ready = sem("idx_ready")
        gathered = [[sem(f"gathered{p}_{g}") for g in range(NG)] for p in range(2)]
        gathers_begun = sem("gathers_begun")
        x_filled = sem("x_filled")
        x_moved = [sem("x_moved_act"), sem("x_moved_dve")]
        gram_filled = sem("gram_filled")
        gram_moved = [sem("gram_moved_act"), sem("gram_moved_dve")]
        tail_filled = sem("tail_filled")
        tail_moved = [sem("tail_moved_act"), sem("tail_moved_dve")]
        stored = sem("stored")
        X_CREDIT = 2 * NG
        GRAM_CREDIT = 2 * UNITS

        block = ctx.enter_context(nc.Block())

        @block.sync
        def _(sp):
            sp.dma_start(ids_sb[:], ids.rearrange("(t p) f -> p t f", p=P)).then_inc(ids_loaded, 16)
            for p in range(2):
                sp.dma_start(rows[p][:, 0, :], dense[p * P:(p + 1) * P, :]).then_inc(dense_loaded[p], 16)
            sp.dma_start(w1a[:], W1[0:D, :]).then_inc(weights_loaded, 16)
            sp.dma_start(w1b[:], W1[D + PAIRS:, :]).then_inc(weights_loaded, 16)
            sp.dma_start(w1p[:], W1[D:D + PAIRS, :].rearrange("(c k) n -> k c n", k=KP)).then_inc(weights_loaded, 16)
            sp.dma_start(w2[:], W2.rearrange("(c p) n -> p c n", p=P)).then_inc(weights_loaded, 16)
            sp.dma_start(w3[:], W3.rearrange("(c p) o -> p (c o)", p=P), allow_slow_non_contiguous=True).then_inc(weights_loaded, 16)
            sp.dma_start(bias1[:], b1.rearrange("(c p) -> p c", p=P), allow_slow_non_contiguous=True).then_inc(weights_loaded, 16)
            sp.dma_start(bias2[:], b2.rearrange("(c p) -> p c", p=P), allow_slow_non_contiguous=True).then_inc(weights_loaded, 16)
            with sp.Fori(1, B // P // 2) as pair:
                for p in range(2):
                    tile = pair * 2 + p
                    sp.wait_ge(x_filled, (tile + 1) * NG)
                    sp.dma_start(rows[p][:, 0, :], dense[bass.ds(tile * P, P), :]).then_inc(dense_loaded[p], 16)
            sp.wait_ge(tail_moved[0], 1 + uses[0] * NM)
            sp.dma_start(out.rearrange("(m g s) o -> g m (s o)", m=NM, s=PER), y[:]).then_inc(stored, 16)
            sp.wait_ge(stored, 16)

        @block.gpsimd
        def _(pool):
            pool.memset(ident[:], 0.0).then_inc(ident_ready, 1)
            pool.wait_ge(ident_ready, 1)
            pool.affine_select(out=ident[:], in_=ident[:], compare_op=ALU.not_equal, fill=1.0, base=0,
                               pattern=[[-1, P]], channel_multiplier=1).then_inc(ident_ready, 1)
            with pool.Fori(0, B // P // 2) as pair:
                for p in range(2):
                    tile = pair * 2 + p
                    pool.wait_ge(x_filled, (tile + 1) * NG)
                    pool.wait_ge(ids_loaded, 16)
                    pool.tensor_copy(idx[p][:], ids_sb[:, tile, :]).then_inc(idx_ready, 1)
                    pool.wait_ge(idx_ready, tile + 1)
                    pool.sem_inc(gathers_begun, 1)
                    for g, features in enumerate(feature_groups):
                        for f in features:
                            if f > 0:
                                pool.indirect_dma_start(
                                    out=rows[p][:, f, :], out_offset=None, in_=tables[f - 1],
                                    in_offset=bass.IndirectOffsetOnAxis(ap=idx[p][:, f - 1:f], axis=0),
                                ).then_inc(gathered[p][g], 16)

        def gathers(g):
            return 16 * sum(f > 0 for f in feature_groups[g])

        @block.tensor
        def _(pe):
            pe.nop().then_inc(x_filled, X_CREDIT)
            pe.nop().then_inc(gram_filled, GRAM_CREDIT)
            pe.wait_ge(ident_ready, 2)
            pe.wait_ge(pads_ready, 2)
            with pe.Fori(0, NM) as m:
                tail_use = [0, 0]

                def tail_bank(q):
                    pe.wait_ge(tail_moved[q % 2], uses[q % 2] * m + (tail_use[q % 2] + 1))
                    tail_use[q % 2] += 1
                    return tail_ps[q % 2]

                def tail_ready(engine, n):
                    pe.wait_ge(tail_moved[engine], uses[engine] * m + (n + 1))

                for t in range(TILES):
                    p = t % 2
                    for g, features in enumerate(feature_groups):
                        k = t * NG + g
                        pe.wait_ge(gathered[p][g], (m * 2 + (t // 2 + 1)) * gathers(g))
                        pe.wait_ge(x_moved[k % 2], m * (TILES * NG // 2) + (k // 2 + 1))
                        if features[0] == 0:
                            pe.wait_ge(dense_loaded[p], (m * 2 + (t // 2 + 1)) * 16)
                        for j, f in enumerate(features):
                            last = pe.transpose(x_ps[k % 2][:, j, :], rows[p][:, f, :], ident[:])
                        last.then_inc(x_filled, 1)
                    for e in range(2):
                        n = (t + 1) * NG
                        pe.wait_ge(x_moved[e], m * (TILES * NG // 2) + ((n + 1 - e) // 2 + 1))
                    for u in range(UNITS):
                        k = t * UNITS + u
                        for e in range(2):
                            pe.wait_ge(gram_moved[e], m * (TILES * UNITS) + (k + 1))
                        for i in range(UNIT):
                            a = PER * (u * UNIT + i)
                            last = pe.matmul(
                                gram_ps[k % 2][:, i // PER_BANK, (i % PER_BANK) * SW:(i % PER_BANK + 1) * SW],
                                x[p][:, a:a + PER, :], x[p][:, a:a + PER, 0:F], start=True, stop=True)
                        last.then_inc(gram_filled, 1)

                for e in range(2):
                    pe.wait_ge(gram_moved[e], (m + 1) * (TILES * UNITS) + 2)
                for q, f0 in enumerate(ZP):
                    bank = tail_bank(q)
                    for j, f in enumerate(range(f0, min(f0 + 4, F - 1))):
                        last = pe.transpose(bank[:, j * P:(j + 1) * P], gram[:, :, f], ident[:])
                    last.then_inc(tail_filled, 1)
                tail_ready(0, (Q_CHUNK + 1) // 2)
                tail_ready(1, Q_CHUNK // 2)
                for c in range(KC):
                    bank = tail_bank(Q_CHUNK + c)
                    for s in range(PER):
                        last = pe.transpose(bank[0:KP, s * P:(s + 1) * P], pairs[:, s, c * KP:(c + 1) * KP], ident[:])
                    last.then_inc(tail_filled, 1)
                pe.wait_ge(dense_w_ready, 1)
                tail_ready(0, (Q_H1 + 1) // 2)
                tail_ready(1, Q_H1 // 2)
                for n in range(N1):
                    bank = tail_bank(Q_H1 + n)
                    cols = slice(n * P, (n + 1) * P)
                    pe.matmul(bank[:], w1d[:, cols], dense_t[:].rearrange("p s g -> p (s g)"), start=True, stop=False)
                    for c in range(KC):
                        last = pe.matmul(bank[:], w1p[:, c, cols], pairs_t[:, c, :], start=False, stop=(c == KC - 1))
                    last.then_inc(tail_filled, 1)
                tail_ready(0, (Q_H2 + 1) // 2)
                tail_ready(1, Q_H2 // 2)
                for n in range(N2):
                    bank = tail_bank(Q_H2 + n)
                    for c in range(N1):
                        last = pe.matmul(bank[:], w2[:, c, n * P:(n + 1) * P], h1[:, c, :],
                                         start=(c == 0), stop=(c == N1 - 1))
                    last.then_inc(tail_filled, 1)
                tail_ready(0, (Q_Y + 1) // 2)
                tail_ready(1, Q_Y // 2)
                bank = tail_bank(Q_Y)
                for s in range(PER):
                    for c in range(N2):
                        last = pe.matmul(bank[:, s:s + 1], h2[:, c, s * P:(s + 1) * P], w3[:, c:c + 1],
                                         start=(c == 0), stop=(c == N2 - 1))
                last.then_inc(tail_filled, 1)

        def move(eng, e):
            def copy(dst, src):
                if e == 0:
                    return eng.activation(dst, src, ACT.Copy)
                return eng.tensor_copy(dst, src)

            def relu(dst, src, bias):
                if e == 0:
                    return eng.activation(dst, src, ACT.Relu, bias=bias)
                return eng.tensor_scalar(dst, src, bias, 0.0, ALU.add, ALU.max)

            with eng.Fori(0, NM) as m:
                for t in range(TILES):
                    p = t % 2
                    eng.wait_ge(gram_filled, m * (TILES * UNITS) + (t + 1) * UNITS)
                    for g, features in enumerate(feature_groups):
                        k = t * NG + g
                        if k % 2 != e:
                            continue
                        n = len(features)
                        eng.wait_ge(x_filled, m * (TILES * NG) + (X_CREDIT + k + 1))
                        if g == 0:
                            copy(dense_t[:, :, t * QUAD:(t + 1) * QUAD],
                                 x_ps[e][:, 0, :].rearrange("p (g s) -> p s g", s=PER))
                        copy(x[p][:, :, features[0]:features[0] + n],
                             x_ps[e][:, 0:n, :].rearrange("p f b -> p b f")).then_inc(x_moved[e], 1)
                    for u in range(UNITS):
                        k = t * UNITS + u
                        eng.wait_ge(gram_filled, m * (TILES * UNITS) + (GRAM_CREDIT + k + 1))
                        for s in (2 * e, 2 * e + 1):
                            rows_s = slice(QUAD * s, QUAD * (s + 1))
                            a = k * UNIT
                            src = gram_ps[k % 2][rows_s, :, 0:PER_BANK * SW]
                            src = src.rearrange("p b (i s f) -> p b i s f", s=PER, f=F)[:, :, :, s, :]
                            dst = gram[rows_s, a:a + UNIT, :].rearrange("p (b i) f -> p b i f", b=UNIT_BANKS)
                            last = copy(dst, src)
                        last.then_inc(gram_moved[e], 1)
                for q in range(e, n_tail, 2):
                    eng.wait_ge(tail_filled, m * n_tail + (q + 1))
                    src = tail_ps[e]
                    if q < Q_CHUNK:
                        for j, f in enumerate(range(ZP[q], min(ZP[q] + 4, F - 1))):
                            block_f = src[:, j * P:(j + 1) * P].rearrange("p (s f) -> p s f", f=QUAD)
                            n = F - 1 - f
                            last = copy(pairs[:, :, first_pair[f]:first_pair[f] + n], block_f[:, :, f + 1:F])
                    elif q < Q_H1:
                        last = copy(pairs_t[:, q - Q_CHUNK, :], src[0:KP, :])
                    elif q < Q_H2:
                        n = q - Q_H1
                        last = relu(h1[:, n, :], src[:], bias1[:, n:n + 1])
                    elif q < Q_Y:
                        n = q - Q_H2
                        last = relu(h2[:, n, :], src[:], bias2[:, n:n + 1])
                    else:
                        last = copy(y[:, m, :], src[:, 0:PER])
                    last.then_inc(tail_moved[e], 1)

        def start_credits(eng, e):
            eng.nop().then_inc(x_moved[e], 1)
            eng.nop().then_inc(gram_moved[e], 2)
            eng.nop().then_inc(tail_moved[e], 1)
            if e == 0:
                eng.wait_ge(pads_ready, 2)
            else:
                for p in range(2):
                    eng.memset(x[p][:, :, F:QUAD], 0.0).then_inc(pads_ready, 1)
            eng.wait_ge(weights_loaded, 16 * 7)

        @block.scalar
        def _(act):
            start_credits(act, 0)
            act.activation(y[:, 0, :], x[0][:, 0, F:F + PER], ACT.Relu)
            move(act, 0)

        @block.vector
        def _(dve):
            start_credits(dve, 1)
            dve.tensor_tensor(w1d[:], w1a[:], w1b[:], ALU.add).then_inc(dense_w_ready, 1)
            move(dve, 1)


NUM_TABLES = 26
_INS = (["r_dense_features", "ids"] + [f"tbl_{f}" for f in range(NUM_TABLES)]
        + ["W_top1", "b_top1", "W_top2", "b_top2", "W_top3"])


def kernel(**inputs):
    import numpy as _np
    import concourse.bacc as _bacc
    from concourse import mybir as _mybir
    from concourse.bass_utils import run_bass_kernel_spmd as _run

    nc = _bacc.Bacc("TRN2", target_bir_lowering=False, num_devices=1)
    arrays, aps = {}, {}
    for name in _INS:
        a = _np.ascontiguousarray(inputs[name])
        arrays[f"in_{name}_dram"] = a
        aps[name] = nc.dram_tensor(f"in_{name}_dram", a.shape, _mybir.dt.from_np(a.dtype), kind="ExternalInput").ap()
    batch = inputs["r_dense_features"].shape[0]
    out = nc.dram_tensor("out_0_dram", (batch, 1), _mybir.dt.float32, kind="ExternalOutput").ap()
    dlrm_kernel(nc, aps["r_dense_features"], aps["ids"], [aps[f"tbl_{f}"] for f in range(NUM_TABLES)],
                aps["W_top1"], aps["b_top1"], aps["W_top2"], aps["b_top2"], aps["W_top3"], out)
    r = _run(nc, [arrays], core_ids=[0])
    return r.results[0]["out_0_dram"]
```

```python
from contextlib import ExitStack

import concourse.bass as bass
from concourse import mybir

F32 = mybir.dt.float32
F32R = mybir.dt.float32r
I32 = mybir.dt.int32
ALU = mybir.AluOpType
ACT = mybir.ActivationFunctionType

P = 128
QUAD = 32
PER = P // QUAD
TILES = 2
BANK = 512

NUM_TABLES = 26
SELECTED = [3, 5, 7, 9, 11, 13]


def runs(features):
    out, i = [], 0
    while i < len(features):
        step = features[i + 1] - features[i] if i + 1 < len(features) else 1
        n = 1
        while i + n < len(features) and features[i + n] - features[i + n - 1] == step:
            n += 1
        out.append((i, features[i], step, n))
        i += n
    return out


def dlrm_kernel(nc: bass.Bass, dense, ids, selected_ids, tables, W1, b1, W2, b2, W3, out):
    B, D = dense.shape
    NT = len(tables)
    F = NT + 1
    H1, H2 = W1.shape[1], W2.shape[1]
    PAIRS = F * (F - 1) // 2
    MACRO = TILES * P
    NM = B // MACRO
    KC = next(k for k in range(1, 9) if PAIRS % k == 0 and PAIRS // k <= P)
    KP = PAIRS // KC
    N1, N2 = H1 // P, H2 // P
    GROUPS = MACRO // PER
    first_pair = [f * F - f * (f + 1) // 2 for f in range(F)]
    assert D == P and F <= QUAD and MACRO <= BANK and (N1, N2) == (4, 2)

    NS = len(SELECTED)
    SROWS = tables[SELECTED[0]].shape[0]
    VC = 8
    VK = SROWS // VC
    assert all(tables[f].shape[0] == SROWS for f in SELECTED) and VK * VC == SROWS and VK <= P
    HALF = VC // 2
    ID_PARTS = [range(0, (NS + 1) // 2), range((NS + 1) // 2, NS)]
    HOTS = 2
    RAWS = P * QUAD // (VC * D)
    PARTS = ("hi", "lo")
    selected_features = [f + 1 for f in SELECTED]
    gathered_features = [f for f in range(F) if f not in selected_features]
    assert gathered_features[0] == 0
    quads = [gathered_features[i:i + 4] for i in range(0, len(gathered_features), 4)]
    if NS % 2:
        feature_groups = [quads, quads[:-1] + [quads[-1][:2], quads[-1][2:]]]
    else:
        feature_groups = [quads, quads]

    UNIT_BANKS = 2
    PER_BANK = 4
    UNIT = UNIT_BANKS * PER_BANK
    UNITS = P // PER // UNIT
    SW = PER * F

    EARLY = 2

    def x_order(ahead):
        def group(t, g0, g1=None):
            return [("rows", t, g) for g in range(len(feature_groups[t]))[g0:g1]]

        def table(*js):
            return [("table", j) for j in js if j < NS and ahead]

        return (group(0, EARLY, 4) + table(0) + group(0, 4) + table(1, 2) + group(1, 0, 4) + table(3)
                + group(1, 4, 5) + table(4) + group(1, 5) + table(5, 6, 7)
                + [("next rows", 0, g) for g in range(EARLY) if ahead])

    X_USES = len(x_order(True))
    assert X_USES % 2 == 0
    LEAD = NS % 2

    def x_base(m):
        return m * X_USES + LEAD + NS + EARLY

    def x_half(m):
        return m * (X_USES // 2) + (LEAD + NS + EARLY) // 2

    def x_use(m, *step):
        if step[:2] == ("rows", 0) and step[2] < EARLY:
            return step[2] - EARLY
        if isinstance(m, int) and m < 0:
            return X_USES - EARLY - NS + step[1]
        return x_order(not isinstance(m, int) or m < NM - 1).index(step)

    def x_last(m, t):
        return x_use(m, "rows", t, len(feature_groups[t]) - 1)

    assert F % 2 == 1 and 2 * GROUPS == P
    pair_banks = [list(range(f, min(f + 8, F - 1), 2)) for f in range(0, F - 1, 8)]
    Q_CHUNK = len(pair_banks)
    Q_H1 = Q_CHUNK + KC
    Q_H2 = Q_H1 + N1
    Q_Y = Q_H2 + N2
    T_USES = Q_Y + 1
    assert T_USES % 2 == 0

    with ExitStack() as ctx:
        def sb(name, shape, dt=F32):
            return ctx.enter_context(nc.sbuf_tensor(name, shape, dt))

        def ps(name, shape):
            return ctx.enter_context(nc.psum_tensor(name, shape, F32))

        def sem(name):
            return ctx.enter_context(nc.semaphore(name))

        ident = sb("ident", [P, P])
        ids_sb = sb("ids_sb", [P, B // P, NT], I32)
        idx = [sb(f"idx{t}", [P, NT], I32) for t in range(TILES)]
        rows = [sb(f"rows{t}", [P, len(gathered_features), D]) for t in range(TILES)]
        x = [sb(f"x{t}", [D, P, QUAD]) for t in range(TILES)]
        dense_new = sb("dense_new", [D, PER, GROUPS])
        dense_t = [sb(f"dense_t_{part}", [D, PER, GROUPS], F32R) for part in PARTS]
        gram = sb("gram", [P, F, GROUPS])
        pairs = sb("pairs", [GROUPS, PER, PAIRS])
        pairs_t = sb("pairs_t", [KP, 2, KC, MACRO], F32R)
        w1d = [sb(f"w1d_{part}", [P, H1], F32R) for part in PARTS]
        w1p = [sb(f"w1p_{part}", [KP, KC, H1], F32R) for part in PARTS]
        w2 = [sb(f"w2_{part}", [P, N1, H2], F32R) for part in PARTS]
        w3 = sb("w3", [P, N2])
        bias1 = sb("bias1", [P, N1])
        bias2 = sb("bias2", [P, N2])
        h1_new = sb("h1_new", [P, 2, MACRO])
        h1 = sb("h1", [P, 2, N1, MACRO], F32R)
        h2 = sb("h2", [P, N2, MACRO])
        y = sb("y", [GROUPS, NM, PER])

        table_hi = [sb(f"table_hi{j}", [VK, VC, D], F32R) for j in range(NS)]
        table_lo = [sb(f"table_lo{j}", [VK, VC, D], F32R) for j in range(NS)]
        x_flat = x[1][:].rearrange("d b f -> d (b f)")
        RAW = VC * D
        table_raw = [x_flat[0:VK, i * RAW:(i + 1) * RAW].rearrange("k (c d) -> k c d", c=VC) for i in range(RAWS)]
        w2_raw = x_flat[:, 0:N1 * H2].rearrange("p (c n) -> p c n", c=N1)
        w1p_raw = x_flat[0:KP, RAW:RAW + KC * H1].rearrange("k (c n) -> k c n", c=KC)
        w1a_raw = h1_new[:].rearrange("p a b -> p (a b)")
        w1b_raw = h2[:].rearrange("p c b -> p (c b)")
        assert NS >= RAWS >= 3 and N1 * H2 <= RAW and KC * H1 <= 2 * RAW and 2 * MACRO == H1 == N2 * MACRO
        row_i = sb("row_i", [P, VC], I32)
        row_f = sb("row_f", [P, VC])
        ids_all = sb("ids_all", [P, NS, MACRO], I32)
        hot = [sb(f"hot{i}", [VK, VC, MACRO], F32R) for i in range(HOTS)]
        picked = sb("picked", [D, NS, MACRO])

        x_ps = [ps(f"x_ps{i}", [P, 4, P]) for i in range(2)]
        gram_ps = [ps(f"gram_ps{i}", [P, UNIT_BANKS, BANK]) for i in range(2)]
        tail_ps = [ps(f"tail_ps{i}", [P, BANK]) for i in range(2)]

        ids_loaded = sem("ids_loaded")
        dense_loaded = [sem(f"dense_loaded{t}") for t in range(TILES)]
        weights_loaded = sem("weights_loaded")
        raw_loaded = [sem(f"raw_loaded{i}") for i in range(RAWS)]
        hi_ready = sem("hi_ready")
        lo_ready = sem("lo_ready")
        ids_all_loaded = [sem(f"ids_all_loaded{h}") for h in range(2)]
        iota_ready = sem("iota_ready")
        rows_ready = sem("rows_ready")
        ident_ready = sem("ident_ready")
        pads_ready = sem("pads_ready")
        w_summed = sem("w_summed")
        w_hi_ready = [sem("w_hi_ready_act"), sem("w_hi_ready_dve")]
        w_lo_ready = sem("w_lo_ready")
        idx_ready = sem("idx_ready")
        gathers_begun = sem("gathers_begun")
        gathered = [[sem(f"gathered{t}_{g}") for g in range(len(feature_groups[t]))] for t in range(TILES)]
        hot_ready = sem("hot_ready")
        x_filled = sem("x_filled")
        x_moved = [sem(f"x_moved{i}") for i in range(2)]
        joined = [sem(f"joined{t}") for t in range(TILES)]
        dense_hi_kept = sem("dense_hi_kept")
        dense_kept = sem("dense_kept")
        pairs_hi_moved = sem("pairs_hi_moved")
        h1_moved = sem("h1_moved")
        h1_split = sem("h1_split")
        gram_filled = sem("gram_filled")
        gram_moved = [sem("gram_moved_act"), sem("gram_moved_dve")]
        tail_begun = sem("tail_begun")
        tail_filled = sem("tail_filled")
        tail_moved = [sem(f"tail_moved{i}") for i in range(2)]
        stored = sem("stored")

        def wait(eng, s, value):
            if not isinstance(value, int) or value > 0:
                eng.wait_ge(s, value)

        block = ctx.enter_context(nc.Block())

        @block.sync
        def _(sp):
            def load_dense(m, t):
                sp.dma_start(rows[t][:, 0, :], dense[bass.ds((m * TILES + t) * P, P), :]).then_inc(dense_loaded[t], 16)

            def load_ids_all(m, h):
                js = slice(ID_PARTS[h][0], ID_PARTS[h][-1] + 1)
                src = selected_ids[js, bass.ds(m * MACRO, MACRO)]
                sp.dma_start(ids_all[:, js, :], src.partition_broadcast(P)).then_inc(ids_all_loaded[h], 16)

            sp.dma_start(ids_sb[:], ids.rearrange("(t p) f -> p t f", p=P)).then_inc(ids_loaded, 16)
            load_ids_all(0, 0)
            for j in range(NS):
                if j >= RAWS:
                    sp.wait_ge(hi_ready, j - RAWS + 1)
                    sp.wait_ge(lo_ready, j - RAWS + 1)
                src = tables[SELECTED[j]].rearrange("(k c) d -> k c d", c=VC)
                sp.dma_start(table_raw[j % RAWS], src).then_inc(raw_loaded[j % RAWS], 16)
                if j == 0:
                    load_ids_all(0, 1)
                elif j <= TILES:
                    load_dense(0, j - 1)
            sp.dma_start(w1a_raw, W1[0:D, :]).then_inc(weights_loaded, 16)
            sp.dma_start(w1b_raw, W1[D + PAIRS:, :]).then_inc(weights_loaded, 16)
            sp.dma_start(w3[:], W3.rearrange("(c p) o -> p (c o)", p=P),
                         allow_slow_non_contiguous=True).then_inc(weights_loaded, 16)
            sp.dma_start(bias1[:], b1.rearrange("(c p) -> p c", p=P),
                         allow_slow_non_contiguous=True).then_inc(weights_loaded, 16)
            sp.dma_start(bias2[:], b2.rearrange("(c p) -> p c", p=P),
                         allow_slow_non_contiguous=True).then_inc(weights_loaded, 16)
            for n, (raw, src) in enumerate(((w2_raw, W2.rearrange("(c p) n -> p c n", p=P)),
                                            (w1p_raw, W1[D:D + PAIRS, :].rearrange("(c k) n -> k c n", k=KP)))):
                taken = max(j for j in range(NS) if j % RAWS in ((0,), (1, 2))[n]) + 1
                sp.wait_ge(hi_ready, taken)
                sp.wait_ge(lo_ready, taken)
                sp.dma_start(raw, src).then_inc(weights_loaded, 16)
            with sp.Fori(1, NM) as m:
                for h in range(2):
                    sp.wait_ge(hot_ready, (m - 1) * (2 * NS) + 2 * (ID_PARTS[h][-1] + 1))
                    load_ids_all(m, h)
                for t in range(TILES):
                    sp.wait_ge(x_filled, x_base(m - 1) + x_last(m - 1, t) + 1)
                    load_dense(m, t)
            sp.wait_ge(tail_moved[Q_Y % 2], 1 + T_USES // 2 * NM)
            sp.dma_start(out.rearrange("(m g s) o -> g m (s o)", m=NM, s=PER), y[:]).then_inc(stored, 16)
            sp.wait_ge(stored, 16)

        @block.gpsimd
        def _(pool):
            def gather(m, t):
                tile = m * TILES + t
                pool.tensor_copy(idx[t][:], ids_sb[:, tile, :]).then_inc(idx_ready, 1)
                pool.wait_ge(idx_ready, tile + 1)
                pool.sem_inc(gathers_begun, 1)
                i = 0
                for g, features in enumerate(feature_groups[t]):
                    for f in features:
                        if f > 0:
                            pool.indirect_dma_start(
                                out=rows[t][:, i, :], out_offset=None, in_=tables[f - 1],
                                in_offset=bass.IndirectOffsetOnAxis(ap=idx[t][:, f - 1:f], axis=0),
                            ).then_inc(gathered[t][g], 16)
                        i += 1

            pool.iota(row_i[:], pattern=[[1, VC]], base=0, channel_multiplier=VC).then_inc(iota_ready, 1)
            pool.memset(ident[:], 0.0).then_inc(ident_ready, 1)
            pool.wait_ge(ident_ready, 1)
            pool.affine_select(out=ident[:], in_=ident[:], compare_op=ALU.not_equal, fill=1.0, base=0,
                               pattern=[[-1, P]], channel_multiplier=1).then_inc(ident_ready, 1)
            pool.wait_ge(ids_loaded, 16)
            for t in range(TILES):
                gather(0, t)
            with pool.Fori(1, NM) as m:
                for t in range(TILES):
                    pool.wait_ge(x_filled, x_base(m - 1) + x_last(m - 1, t) + 1)
                    gather(m, t)

        @block.tensor
        def _(pe):
            def x_bank(m, k):
                n = x_half(m) + k // 2
                wait(pe, x_moved[k % 2], n)
                return x_ps[k % 2]

            def transposes(m, t, g0, g1):
                for g in range(g0, g1):
                    features = feature_groups[t][g]
                    pe.wait_ge(gathered[t][g], (m + 1) * 16 * sum(f > 0 for f in features))
                    if features[0] == 0:
                        pe.wait_ge(dense_loaded[t], (m + 1) * 16)
                    bank = x_bank(m, x_use(m, "rows", t, g))
                    for j, f in enumerate(features):
                        last = pe.transpose(bank[:, j, :], rows[t][:, gathered_features.index(f), :], ident[:])
                    last.then_inc(x_filled, 1)

            def select(m, j):
                if j >= NS:
                    return
                if isinstance(m, int) and m < 0:
                    pe.wait_ge(hi_ready, j + 1)
                    pe.wait_ge(lo_ready, j + 1)
                bank = x_bank(m, x_use(m, "table", j))[:].rearrange("p a b -> p (a b)")[:, 0:MACRO]
                for c in range(VC):
                    if c % HALF == 0:
                        pe.wait_ge(hot_ready, (m + 1) * (2 * NS) + (2 * j + c // HALF + 1))
                    for part in (table_hi, table_lo):
                        last = pe.matmul(bank, part[j][:, c, :], hot[j % HOTS][:, c, :],
                                         start=(c == 0 and part is table_hi),
                                         stop=(c == VC - 1 and part is table_lo))
                last.then_inc(x_filled, 1)

            def gram_products(m, t, u):
                if u == 0:
                    if isinstance(m, int) and m == 0:
                        pe.wait_ge(pads_ready, t + 1)
                    for i in range(2):
                        pe.wait_ge(x_moved[i], x_half(m) + (x_last(m, t) + 2 - i) // 2)
                    pe.wait_ge(joined[t], m + 1)
                k = t * UNITS + u
                for e in range(2):
                    wait(pe, gram_moved[e], m * (TILES * UNITS) + (k - 1))
                for i in range(UNIT):
                    a = PER * (u * UNIT + i)
                    last = pe.matmul(
                        gram_ps[k % 2][:, i // PER_BANK, (i % PER_BANK) * SW:(i % PER_BANK + 1) * SW],
                        x[t][:, a:a + PER, :], x[t][:, a:a + PER, 0:F], start=True, stop=True)
                last.then_inc(gram_filled, 1)

            def tail_bank(m, q):
                pe.wait_ge(tail_moved[q % 2], m * (T_USES // 2) + (q // 2 + 1))
                return tail_ps[q % 2]

            def tail_ready(m, q):
                pe.wait_ge(tail_moved[0], m * (T_USES // 2) + ((q + 1) // 2 + 1))
                pe.wait_ge(tail_moved[1], m * (T_USES // 2) + (q // 2 + 1))

            def pair_transposes(m, q0, q1):
                if q0 == 0:
                    for e in range(2):
                        pe.wait_ge(gram_moved[e], (m + 1) * (TILES * UNITS))
                for q in range(q0, q1):
                    bank = tail_bank(m, q)
                    for j, f in enumerate(pair_banks[q]):
                        last = pe.transpose(bank[:, j * P:(j + 1) * P],
                                            gram[:, f:f + 2, :].rearrange("p f g -> p (f g)"), ident[:])
                    last.then_inc(tail_filled, 1)

            def chunk_transposes(m, c0, c1):
                if c0 == 0:
                    tail_ready(m, Q_CHUNK)
                for c in range(c0, c1):
                    bank = tail_bank(m, Q_CHUNK + c)
                    pe.sem_inc(tail_begun, 1)
                    for s in range(PER):
                        last = pe.transpose(bank[0:KP, s * GROUPS:(s + 1) * GROUPS],
                                            pairs[:, s, c * KP:(c + 1) * KP], ident[0:GROUPS, 0:GROUPS])
                    last.then_inc(tail_filled, 1)

            def product(bank, operands):
                steps = [(w[a], v[b]) for w, v in operands for a, b in ((0, 0), (0, 1), (1, 0))]
                for i, (w, v) in enumerate(steps):
                    last = pe.matmul(bank, w, v, start=(i == 0), stop=(i == len(steps) - 1))
                last.then_inc(tail_filled, 1)

            def layer1(m, n):
                if n == 0:
                    tail_ready(m, Q_H1)
                    pe.wait_ge(dense_kept, m + 1)
                bank = tail_bank(m, Q_H1 + n)[:, 0:MACRO]
                cols = slice(n * P, (n + 1) * P)
                operands = [([w[:, cols] for w in w1d], [v[:].rearrange("p s g -> p (s g)") for v in dense_t])]
                operands += [([w[:, c, cols] for w in w1p], [pairs_t[:, i, c, :] for i in range(2)])
                             for c in range(KC)]
                product(bank, operands)

            def layer2(m, n):
                if n == 0:
                    pe.wait_ge(h1_split, 1 + (m + 1) * N1)
                bank = tail_bank(m, Q_H2 + n)[:, 0:MACRO]
                cols = slice(n * P, (n + 1) * P)
                product(bank, [([w[:, c, cols] for w in w2], [h1[:, i, c, :] for i in range(2)])
                               for c in range(N1)])

            def layer3(m):
                tail_ready(m, Q_Y)
                bank = tail_bank(m, Q_Y)
                for s in range(PER):
                    for c in range(N2):
                        last = pe.matmul(bank[0:GROUPS, s:s + 1], h2[:, c, s * GROUPS:(s + 1) * GROUPS],
                                         w3[:, c:c + 1], start=(c == 0), stop=(c == N2 - 1))
                last.then_inc(tail_filled, 1)

            def macro_tile(m, before, ahead):
                transposes(m, 0, EARLY, 4)
                if before:
                    pair_transposes(m - 1, 0, 2)
                if ahead:
                    select(m, 0)
                if before:
                    pair_transposes(m - 1, 2, Q_CHUNK)
                transposes(m, 0, 4, len(feature_groups[0]))
                if ahead:
                    select(m, 1)
                if before:
                    chunk_transposes(m - 1, 0, 2)
                if ahead:
                    select(m, 2)
                gram_products(m, 0, 0)
                if before:
                    chunk_transposes(m - 1, 2, KC)
                for u in range(1, UNITS):
                    transposes(m, 1, u - 1, u)
                    gram_products(m, 0, u)
                    if before:
                        layer1(m - 1, u - 1)
                transposes(m, 1, 3, 4)
                if ahead:
                    select(m, 3)
                if before:
                    layer1(m - 1, 3)
                transposes(m, 1, 4, 5)
                if ahead:
                    select(m, 4)
                transposes(m, 1, 5, len(feature_groups[1]))
                if before:
                    layer2(m - 1, 0)
                gram_products(m, 1, 0)
                if before:
                    layer2(m - 1, 1)
                gram_products(m, 1, 1)
                if ahead:
                    select(m, 5)
                if before:
                    layer3(m - 1)
                if ahead:
                    select(m, 6)
                gram_products(m, 1, 2)
                if ahead:
                    select(m, 7)
                    transposes(m + 1, 0, 0, 1)
                gram_products(m, 1, 3)
                if ahead:
                    transposes(m + 1, 0, 1, EARLY)

            if LEAD:
                pe.nop().then_inc(x_filled, 1)
            for j in range(NS):
                select(-1, j)
            pe.wait_ge(ident_ready, 2)
            transposes(0, 0, 0, EARLY)
            macro_tile(0, False, True)
            pe.wait_ge(w_lo_ready, 3)
            with pe.Fori(1, NM - 1) as m:
                macro_tile(m, True, True)
            macro_tile(NM - 1, True, False)
            pair_transposes(NM - 1, 0, Q_CHUNK)
            chunk_transposes(NM - 1, 0, KC)
            for n in range(N1):
                layer1(NM - 1, n)
            for n in range(N2):
                layer2(NM - 1, n)
            layer3(NM - 1)

        def gram_quadrants(copy, e, k):
            for s in (2 * e, 2 * e + 1):
                rows_s = slice(QUAD * s, QUAD * (s + 1))
                src = gram_ps[k % 2][rows_s, :, 0:PER_BANK * SW]
                src = src.rearrange("p b (i s f) -> p b i s f", s=PER, f=F)[:, :, :, s, :]
                dst = gram[rows_s, :, k * UNIT:(k + 1) * UNIT]
                last = copy(dst.rearrange("p f (b i) -> p b i f", b=UNIT_BANKS), src)
            return last

        def pair_columns(copy, q):
            for j, f0 in enumerate(pair_banks[q]):
                for i in range(2):
                    f = f0 + i
                    block_f = tail_ps[q % 2][i * GROUPS:(i + 1) * GROUPS, j * P:(j + 1) * P]
                    n = F - 1 - f
                    last = copy(pairs[:, :, first_pair[f]:first_pair[f] + n],
                                block_f.rearrange("p (s f) -> p s f", f=QUAD)[:, :, f + 1:F])
            return last

        @block.scalar
        def _(act):
            def copy(dst, src):
                return act.activation(dst, src, ACT.Copy)

            def transposes(m, t, g0, g1):
                for g in range(g0, g1):
                    features = feature_groups[t][g]
                    k = x_use(m, "rows", t, g)
                    act.wait_ge(x_filled, x_base(m) + (k + 1))
                    if g == 0:
                        wait(act, dense_kept, m)
                        copy(dense_new[:, :, t * QUAD:(t + 1) * QUAD],
                             x_ps[k % 2][:, 0, :].rearrange("p (g s) -> p s g", s=PER))
                    for i, f, step, n in runs(features):
                        last = copy(x[t][:, :, f:f + (n - 1) * step + 1:step],
                                    x_ps[k % 2][:, i:i + n, :].rearrange("p f b -> p b f"))
                    last.then_inc(x_moved[k % 2], 1)

            def select(m, j):
                if j >= NS:
                    return
                if not (isinstance(m, int) and m < 0):
                    act.wait_ge(joined[1], m + 1)
                k = x_use(m, "table", j)
                act.wait_ge(x_filled, x_base(m) + (k + 1))
                src = x_ps[k % 2][:].rearrange("p a b -> p (a b)")[:, 0:MACRO]
                copy(picked[:, j, :], src).then_inc(x_moved[k % 2], 1)

            def join(m, t):
                wait(act, gram_filled, (m - 1) * (TILES * UNITS) + (t + 1) * UNITS)
                for i in range(2):
                    act.wait_ge(x_moved[i], x_half(m) - EARLY // 2)
                for i, f, step, n in runs(selected_features):
                    last = copy(x[t][:, :, f:f + (n - 1) * step + 1:step],
                                picked[:, i:i + n, t * P:(t + 1) * P].rearrange("p f b -> p b f"))
                last.then_inc(joined[t], 1)

            def keep_dense(m):
                for t in range(TILES):
                    k = x_use(m, "rows", t, 0)
                    act.wait_ge(x_moved[k % 2], x_half(m) + (k // 2 + 1))
                copy(dense_t[0][:], dense_new[:]).then_inc(dense_hi_kept, 1)

            def gram_products(m, t, u):
                k = t * UNITS + u
                act.wait_ge(gram_filled, m * (TILES * UNITS) + (k + 1))
                gram_quadrants(copy, 0, k).then_inc(gram_moved[0], 1)

            def pair_transposes(m, q):
                act.wait_ge(tail_filled, m * T_USES + (q + 1))
                pair_columns(copy, q).then_inc(tail_moved[0], 1)

            def chunk_transposes(m, c0, c1):
                for c in range(c0, c1):
                    q = Q_CHUNK + c
                    act.wait_ge(tail_filled, m * T_USES + (q + 1))
                    copy(pairs_t[:, 0, c, :], tail_ps[q % 2][0:KP, 0:MACRO]).then_inc(pairs_hi_moved, 1)

            def layer1(m, n):
                q = Q_H1 + n
                act.wait_ge(tail_filled, m * T_USES + (q + 1))
                act.wait_ge(h1_split, m * N1 + n)
                src = tail_ps[q % 2][:, 0:MACRO]
                act.activation(h1_new[:, n % 2, :], src, ACT.Relu, bias=bias1[:, n:n + 1]).then_inc(h1_moved, 1)
                act.activation(h1[:, 0, n, :], src, ACT.Relu, bias=bias1[:, n:n + 1]).then_inc(tail_moved[q % 2], 1)

            def layer2(m, n):
                q = Q_H2 + n
                act.wait_ge(tail_filled, m * T_USES + (q + 1))
                act.activation(h2[:, n, :], tail_ps[q % 2][:, 0:MACRO], ACT.Relu,
                               bias=bias2[:, n:n + 1]).then_inc(tail_moved[q % 2], 1)

            def layer3(m):
                act.wait_ge(tail_filled, m * T_USES + (Q_Y + 1))
                copy(y[:, m, :], tail_ps[Q_Y % 2][0:GROUPS, 0:PER]).then_inc(tail_moved[Q_Y % 2], 1)

            def macro_tile(m, before, ahead):
                if not before:
                    act.wait_ge(lo_ready, NS)
                    act.wait_ge(w_lo_ready, 3)
                transposes(m, 0, EARLY, 4)
                if before:
                    pair_transposes(m - 1, 0)
                join(m, 1)
                if ahead:
                    select(m, 0)
                if before:
                    pair_transposes(m - 1, 2)
                transposes(m, 0, 4, len(feature_groups[0]))
                if ahead:
                    select(m, 1)
                if before:
                    chunk_transposes(m - 1, 0, 2)
                if ahead:
                    select(m, 2)
                gram_products(m, 0, 0)
                if before:
                    chunk_transposes(m - 1, 2, KC)
                for u in range(1, UNITS):
                    transposes(m, 1, u - 1, u)
                    gram_products(m, 0, u)
                    if before:
                        layer1(m - 1, u - 1)
                transposes(m, 1, 3, 4)
                if ahead:
                    select(m, 3)
                if before:
                    layer1(m - 1, 3)
                transposes(m, 1, 4, 5)
                if ahead:
                    select(m, 4)
                transposes(m, 1, 5, len(feature_groups[1]))
                if before:
                    layer2(m - 1, 0)
                gram_products(m, 1, 0)
                keep_dense(m)
                if before:
                    layer2(m - 1, 1)
                gram_products(m, 1, 1)
                if ahead:
                    select(m, 5)
                if before:
                    layer3(m - 1)
                if ahead:
                    select(m, 6)
                gram_products(m, 1, 2)
                if ahead:
                    select(m, 7)
                    join(m + 1, 0)
                    transposes(m + 1, 0, 0, 1)
                gram_products(m, 1, 3)
                if ahead:
                    transposes(m + 1, 0, 1, EARLY)

            act.nop().then_inc(tail_moved[0], 1)
            if LEAD:
                act.nop().then_inc(x_moved[0], 1)
            for j in range(NS):
                act.wait_ge(raw_loaded[j % RAWS], 16 * (j // RAWS + 1))
                copy(table_hi[j][:], table_raw[j % RAWS]).then_inc(hi_ready, 1)
                if j > 0:
                    select(-1, j - 1)
            select(-1, NS - 1)
            act.wait_ge(weights_loaded, 16 * 7)
            copy(w1p[0][:], w1p_raw)
            copy(w2[0][:], w2_raw).then_inc(w_hi_ready[0], 1)
            join(0, 0)
            transposes(0, 0, 0, EARLY)
            macro_tile(0, False, True)
            with act.Fori(1, NM - 1) as m:
                macro_tile(m, True, True)
            macro_tile(NM - 1, True, False)
            for q in range(0, Q_CHUNK, 2):
                pair_transposes(NM - 1, q)
            chunk_transposes(NM - 1, 0, KC)
            for n in range(N1):
                layer1(NM - 1, n)
            for n in range(N2):
                layer2(NM - 1, n)
            layer3(NM - 1)

        @block.vector
        def _(dve):
            def copy(dst, src):
                return dve.tensor_copy(dst, src)

            def low_part(lo, whole, hi):
                return dve.tensor_tensor(lo, whole, hi.bitcast(F32), ALU.subtract)

            def selected(m, j):
                if isinstance(m, int) and m == 0:
                    return LEAD + j + 1
                return x_base(m - 1) + (x_use(m - 1, "table", j) + 1)

            def build_hot(m, j, c0=0, c1=VC):
                if j >= NS:
                    return
                if c0 == 0:
                    dve.wait_ge(ids_all_loaded[0 if j in ID_PARTS[0] else 1], (m + 1) * 16)
                    if j >= HOTS:
                        dve.wait_ge(x_filled, selected(m, j - HOTS))
                    elif not (isinstance(m, int) and m == 0):
                        dve.wait_ge(x_filled, selected(m - 1, NS - HOTS + j))
                for c in range(c0, c1):
                    last = dve.tensor_scalar(hot[j % HOTS][:, c, :], ids_all[0:VK, j, :],
                                             row_f[0:VK, c:c + 1], None, ALU.is_equal)
                    if c % HALF == HALF - 1:
                        last.then_inc(hot_ready, 1)

            def keep_dense(m):
                dve.wait_ge(dense_hi_kept, m + 1)
                low_part(dense_t[1][:], dense_new[:], dense_t[0][:]).then_inc(dense_kept, 1)

            def gram_products(m, k):
                dve.wait_ge(gram_filled, m * (TILES * UNITS) + (k + 1))
                gram_quadrants(copy, 1, k).then_inc(gram_moved[1], 1)

            def pair_transposes(m, q):
                dve.wait_ge(tail_filled, m * T_USES + (q + 1))
                pair_columns(copy, q).then_inc(tail_moved[1], 1)

            def chunk_transposes(m, c0, c1):
                for c in range(c0, c1):
                    q = Q_CHUNK + c
                    dve.wait_ge(pairs_hi_moved, m * KC + (c + 1))
                    low_part(pairs_t[:, 1, c, :], tail_ps[q % 2][0:KP, 0:MACRO],
                             pairs_t[:, 0, c, :]).then_inc(tail_moved[q % 2], 1)

            def layer1(m, n):
                dve.wait_ge(h1_moved, m * N1 + (n + 1))
                dve.wait_ge(tail_moved[(Q_H1 + n) % 2], m * (T_USES // 2) + ((Q_H1 + n) // 2 + 2))
                low_part(h1[:, 1, n, :], h1_new[:, n % 2, :], h1[:, 0, n, :]).then_inc(h1_split, 1)

            def macro_tile(m, before, ahead):
                hots = build_hot if ahead else lambda *a: None
                if not before:
                    split_weights()
                hots(m + 1, 0)
                if before:
                    pair_transposes(m - 1, 1)
                hots(m + 1, 1, 0, HALF)
                if before:
                    pair_transposes(m - 1, 3)
                hots(m + 1, 1, HALF, VC)
                hots(m + 1, 2)
                if before:
                    chunk_transposes(m - 1, 0, 2)
                gram_products(m, 0)
                if before:
                    chunk_transposes(m - 1, 2, KC)
                gram_products(m, 1)
                if before:
                    layer1(m - 1, 0)
                hots(m + 1, 3, 0, HALF)
                gram_products(m, 2)
                if before:
                    layer1(m - 1, 1)
                hots(m + 1, 3, HALF, VC)
                gram_products(m, 3)
                if before:
                    layer1(m - 1, 2)
                hots(m + 1, 4)
                if before:
                    layer1(m - 1, 3)
                hots(m + 1, 5, 0, HALF)
                gram_products(m, UNITS)
                keep_dense(m)
                hots(m + 1, 5, HALF, VC)
                gram_products(m, UNITS + 1)
                hots(m + 1, 6)
                hots(m + 1, 7)
                gram_products(m, UNITS + 2)
                gram_products(m, UNITS + 3)

            def split_weights():
                dve.wait_ge(weights_loaded, 16 * 7)
                dve.tensor_tensor(w1a_raw, w1a_raw, w1b_raw, ALU.add).then_inc(w_summed, 1)
                dve.wait_ge(w_summed, 1)
                copy(w1d[0][:], w1a_raw).then_inc(w_hi_ready[1], 1)
                dve.wait_ge(w_hi_ready[0], 1)
                low_part(w1p[1][:], w1p_raw, w1p[0][:]).then_inc(w_lo_ready, 1)
                low_part(w2[1][:], w2_raw, w2[0][:]).then_inc(w_lo_ready, 1)
                dve.wait_ge(w_hi_ready[1], 1)
                low_part(w1d[1][:], w1a_raw, w1d[0][:]).then_inc(w_lo_ready, 1)
                dve.wait_ge(lo_ready, NS)
                dve.wait_ge(w_lo_ready, 3)
                dve.memset(x[1][:, :, F:QUAD], 0.0).then_inc(pads_ready, 1)

            dve.nop().then_inc(tail_moved[1], 1)
            dve.nop().then_inc(h1_split, 1)
            dve.memset(x[0][:, :, F:QUAD], 0.0).then_inc(pads_ready, 1)
            dve.wait_ge(iota_ready, 1)
            copy(row_f[:], row_i[:]).then_inc(rows_ready, 1)
            dve.wait_ge(rows_ready, 1)
            for j in range(NS):
                build_hot(0, j)
                dve.wait_ge(hi_ready, j + 1)
                low_part(table_lo[j][:], table_raw[j % RAWS], table_hi[j][:]).then_inc(lo_ready, 1)
            macro_tile(0, False, True)
            with dve.Fori(1, NM - 1) as m:
                macro_tile(m, True, True)
            macro_tile(NM - 1, True, False)
            for q in range(1, Q_CHUNK, 2):
                pair_transposes(NM - 1, q)
            chunk_transposes(NM - 1, 0, KC)
            for n in range(N1):
                layer1(NM - 1, n)


_INS = (["r_dense_features", "ids"] + [f"tbl_{f}" for f in range(NUM_TABLES)]
        + ["W_top1", "b_top1", "W_top2", "b_top2", "W_top3"])


def kernel(**inputs):
    import numpy as _np
    import concourse.bacc as _bacc
    from concourse import mybir as _mybir
    from concourse.bass_utils import run_bass_kernel_spmd as _run

    nc = _bacc.Bacc("TRN2", target_bir_lowering=False, num_devices=1)
    given = {name: _np.ascontiguousarray(inputs[name]) for name in _INS}
    given["selected_ids"] = _np.ascontiguousarray(given["ids"].T[SELECTED])
    arrays, aps = {}, {}
    for name, a in given.items():
        arrays[f"in_{name}_dram"] = a
        aps[name] = nc.dram_tensor(f"in_{name}_dram", a.shape, _mybir.dt.from_np(a.dtype), kind="ExternalInput").ap()
    batch = inputs["r_dense_features"].shape[0]
    out = nc.dram_tensor("out_0_dram", (batch, 1), _mybir.dt.float32, kind="ExternalOutput").ap()
    dlrm_kernel(nc, aps["r_dense_features"], aps["ids"], aps["selected_ids"],
                [aps[f"tbl_{f}"] for f in range(NUM_TABLES)],
                aps["W_top1"], aps["b_top1"], aps["W_top2"], aps["b_top2"], aps["W_top3"], out)
    r = _run(nc, [arrays], core_ids=[0])
    return r.results[0]["out_0_dram"]
```

```python
from contextlib import ExitStack

import concourse.bass as bass
from concourse import mybir

F32 = mybir.dt.float32
F32R = mybir.dt.float32r
I32 = mybir.dt.int32
ALU = mybir.AluOpType
ACT = mybir.ActivationFunctionType

P = 128
QUAD = 32
PER = P // QUAD
TILES = 2
BANK = 512

NUM_TABLES = 26
SELECTED = [3, 5, 7, 9, 11, 13, 6]
EXTRA = 4


def runs(features):
    out, i = [], 0
    while i < len(features):
        step = features[i + 1] - features[i] if i + 1 < len(features) else 1
        step = step if step > 0 else 1
        n = 1
        while i + n < len(features) and features[i + n] - features[i + n - 1] == step:
            n += 1
        out.append((i, features[i], step, n))
        i += n
    return out


def dlrm_kernel(nc: bass.Bass, dense, ids, selected_ids, tables, W1, b1, W2, b2, W3, out):
    B, D = dense.shape
    NT = len(tables)
    F = NT + 1
    H1, H2 = W1.shape[1], W2.shape[1]
    PAIRS = F * (F - 1) // 2
    MACRO = TILES * P
    NM = B // MACRO
    KC = next(k for k in range(1, 9) if PAIRS % k == 0 and PAIRS // k <= P)
    KP = PAIRS // KC
    N1, N2 = H1 // P, H2 // P
    GROUPS = MACRO // PER
    first_pair = [f * F - f * (f + 1) // 2 for f in range(F)]
    assert D == P and F <= QUAD and MACRO <= BANK and (N1, N2) == (4, 2)

    NS = len(SELECTED)
    SROWS = tables[SELECTED[0]].shape[0]
    VC = 8
    VK = SROWS // VC
    assert all(tables[f].shape[0] == SROWS for f in SELECTED) and VK * VC == SROWS and VK <= P
    HALF = VC // 2
    ID_PARTS = [range(0, 2), range(2, NS)]
    HOTS = 2
    RAWS = P * QUAD // (VC * D)
    PARTS = ("hi", "lo")
    selected_features = [f + 1 for f in SELECTED]
    gathered_features = [f for f in range(F) if f not in selected_features]
    assert gathered_features[0] == 0
    quads = [gathered_features[i:i + 4] for i in range(0, len(gathered_features), 4)]
    feature_groups = [quads, quads[:-1] + [quads[-1][:2], quads[-1][2:]] if NS % 2 else quads]
    extra_features = selected_features[NS - EXTRA:]
    extra_groups = [extra_features[i:i + 4] for i in range(0, EXTRA, 4)]

    UNIT_BANKS = 2
    PER_BANK = 4
    UNIT = UNIT_BANKS * PER_BANK
    UNITS = P // PER // UNIT
    SW = PER * F

    EARLY = 2

    def is_last(m):
        return isinstance(m, int) and m == NM - 1

    def num_selected(m):
        return NS - EXTRA if is_last(m) else NS

    def groups(m, t):
        return feature_groups[t] + (extra_groups if is_last(m) else [])

    def x_order(m):
        def group(t, g0, g1=None):
            return [("rows", t, g) for g in range(len(groups(m, t)))[g0:g1]]

        def table(*js):
            return [("table", j) for j in js if not is_last(m) and j < num_selected(m + 1)]

        return (group(0, EARLY, 4) + table(0) + group(0, 4) + table(1, 2) + group(1, 0, 4) + table(3)
                + group(1, 4, 5) + table(4) + group(1, 5) + table(5, 6, 7)
                + [("next rows", 0, g) for g in range(EARLY) if not is_last(m)])

    X_USES = len(x_order(0))
    assert X_USES % 2 == 0

    def x_before(m, k, i=None):
        first = NS + EARLY + k - (EXTRA if is_last(m) else 0)
        return m * X_USES + first if i is None else m * (X_USES // 2) + (first + 1 - i) // 2

    def x_use(m, *step):
        if step[:2] == ("rows", 0) and step[2] < EARLY:
            return step[2] - EARLY
        if isinstance(m, int) and m < 0:
            return X_USES - EARLY - NS + step[1]
        return x_order(m).index(step)

    def x_bank_of(m, k):
        return (NS + EARLY + k - (EXTRA if is_last(m) else 0)) % 2

    def x_end(m, t):
        return x_use(m, "rows", t, len(groups(m, t)) - 1) + 1

    assert F % 2 == 1 and 2 * GROUPS == P
    pair_banks = [list(range(f, min(f + 8, F - 1), 2)) for f in range(0, F - 1, 8)]
    Q_CHUNK = len(pair_banks)
    Q_H1 = Q_CHUNK + KC
    Q_H2 = Q_H1 + N1
    Q_Y = Q_H2 + N2
    T_USES = Q_Y + 1
    assert T_USES % 2 == 0

    def tail_at(m, q):
        if is_last(m):
            return q % 4, m * (T_USES // 2) + (q // 4 + 1) if q % 4 < 2 else q // 4
        return q % 2, m * (T_USES // 2) + (q // 2 + 1)

    with ExitStack() as ctx:
        def sb(name, shape, dt=F32):
            return ctx.enter_context(nc.sbuf_tensor(name, shape, dt))

        def ps(name, shape):
            return ctx.enter_context(nc.psum_tensor(name, shape, F32))

        def sem(name):
            return ctx.enter_context(nc.semaphore(name))

        ident = sb("ident", [P, P])
        ids_sb = sb("ids_sb", [P, B // P, NT], I32)
        idx = [sb(f"idx{t}", [P, NT], I32) for t in range(TILES)]
        rows = [sb(f"rows{t}", [P, len(gathered_features), D]) for t in range(TILES)]
        x = [sb(f"x{t}", [D, P, QUAD]) for t in range(TILES)]
        dense_new = sb("dense_new", [D, PER, GROUPS])
        dense_t = [sb(f"dense_t_{part}", [D, PER, GROUPS], F32R) for part in PARTS]
        gram = sb("gram", [P, F, GROUPS])
        pairs = sb("pairs", [GROUPS, PER, PAIRS])
        pairs_t = sb("pairs_t", [KP, 2, KC, MACRO], F32R)
        w1d = [sb(f"w1d_{part}", [P, H1], F32R) for part in PARTS]
        w1p = [sb(f"w1p_{part}", [KP, KC, H1], F32R) for part in PARTS]
        w2 = [sb(f"w2_{part}", [P, N1, H2], F32R) for part in PARTS]
        w3 = sb("w3", [P, N2])
        bias1 = sb("bias1", [P, N1])
        bias2 = sb("bias2", [P, N2])
        h1_new = sb("h1_new", [P, 2, MACRO])
        h1 = sb("h1", [P, 2, N1, MACRO], F32R)
        h2 = sb("h2", [P, N2, MACRO])
        y = sb("y", [GROUPS, NM, PER])

        table_hi = [sb(f"table_hi{j}", [VK, VC, D], F32R) for j in range(NS)]
        table_lo = [sb(f"table_lo{j}", [VK, VC, D], F32R) for j in range(NS)]
        picked = sb("picked", [D, NS, MACRO])
        x_flat = x[1][:].rearrange("d b f -> d (b f)")
        RAW = VC * D
        table_raw = [x_flat[0:VK, i * RAW:(i + 1) * RAW].rearrange("k (c d) -> k c d", c=VC) for i in range(RAWS)]
        w1p_raw = sb("w1p_raw", [KP, KC, H1])
        w2_raw = gram[:].rearrange("p f g -> p (f g)")[:, 0:N1 * H2].rearrange("p (c n) -> p c n", c=N1)
        w1a_raw = h1_new[:].rearrange("p a b -> p (a b)")
        w1b_raw = h2[:].rearrange("p c b -> p (c b)")
        assert N1 * H2 <= F * GROUPS and 2 * MACRO == H1 == N2 * MACRO
        picked_flat = picked[:].rearrange("d j b -> d (j b)")
        extra_at = [(NS - EXTRA) * MACRO + t * EXTRA * D for t in range(TILES)]
        extra_rows = [picked_flat[:, a:a + EXTRA * D].rearrange("p (j d) -> p j d", j=EXTRA) for a in extra_at]
        row_i = sb("row_i", [P, VC], I32)
        row_f = sb("row_f", [P, VC])
        ids_all = sb("ids_all", [P, NS, MACRO], I32)
        hot = [sb(f"hot{i}", [VK, VC, MACRO], F32R) for i in range(HOTS)]

        x_ps = [ps(f"x_ps{i}", [P, 4, P]) for i in range(2)]
        gram_ps = [ps(f"gram_ps{i}", [P, UNIT_BANKS, BANK]) for i in range(2)]
        tail_ps = [ps(f"tail_ps{i}", [P, BANK]) for i in range(2)]
        tail_banks = tail_ps + [b[:].rearrange("p a b -> p (a b)") for b in x_ps]

        ids_loaded = [sem("ids_loaded_first"), sem("ids_loaded_rest")]
        dense_loaded = [sem(f"dense_loaded{t}") for t in range(TILES)]
        weights_loaded = sem("weights_loaded")
        raw_loaded = [sem(f"raw_loaded{i}") for i in range(RAWS)]
        hi_ready = sem("hi_ready")
        lo_ready = sem("lo_ready")
        ids_all_loaded = [sem(f"ids_all_loaded{h}") for h in range(2)]
        iota_ready = sem("iota_ready")
        rows_ready = sem("rows_ready")
        ident_ready = sem("ident_ready")
        pads_ready = sem("pads_ready")
        w_summed = sem("w_summed")
        w_hi_ready = [sem("w_hi_ready_act"), sem("w_hi_ready_dve")]
        w_lo_ready = sem("w_lo_ready")
        idx_ready = sem("idx_ready")
        extra_gathered = [[sem(f"extra_gathered{t}_{g}") for g in range(len(extra_groups))] for t in range(TILES)]
        gathers_begun = sem("gathers_begun")
        gathered = [[sem(f"gathered{t}_{g}") for g in range(len(feature_groups[t]))] for t in range(TILES)]
        hot_ready = sem("hot_ready")
        x_filled = sem("x_filled")
        x_moved = [sem(f"x_moved{i}") for i in range(2)]
        joined = [sem(f"joined{t}") for t in range(TILES)]
        dense_hi_kept = sem("dense_hi_kept")
        dense_kept = sem("dense_kept")
        pairs_hi_moved = sem("pairs_hi_moved")
        h1_moved = sem("h1_moved")
        h1_split = sem("h1_split")
        gram_filled = sem("gram_filled")
        gram_moved = [sem("gram_moved_act"), sem("gram_moved_dve")]
        tail_begun = sem("tail_begun")
        tail_filled = sem("tail_filled")
        tail_moved = [sem(f"tail_moved{i}") for i in range(4)]
        stored = sem("stored")

        def wait_tail_moved(eng, m, q):
            i, n = tail_at(m, q)
            eng.wait_ge(tail_moved[i], n + 1)

        def wait(eng, s, value):
            if not isinstance(value, int) or value > 0:
                eng.wait_ge(s, value)

        block = ctx.enter_context(nc.Block())

        @block.sync
        def _(sp):
            def load_dense(m, t):
                sp.dma_start(rows[t][:, 0, :], dense[bass.ds((m * TILES + t) * P, P), :]).then_inc(dense_loaded[t], 16)

            def load_ids_all(m, h):
                js = slice(ID_PARTS[h][0], ID_PARTS[h][-1] + 1)
                src = selected_ids[js, bass.ds(m * MACRO, MACRO)]
                sp.dma_start(ids_all[:, js, :], src.partition_broadcast(P)).then_inc(ids_all_loaded[h], 16)

            def load_weights():
                sp.dma_start(w1a_raw, W1[0:D, :]).then_inc(weights_loaded, 16)
                sp.dma_start(w1b_raw, W1[D + PAIRS:, :]).then_inc(weights_loaded, 16)
                sp.dma_start(w1p_raw[:], W1[D:D + PAIRS, :].rearrange("(c k) n -> k c n", k=KP)).then_inc(weights_loaded, 16)
                sp.dma_start(w2_raw, W2.rearrange("(c p) n -> p c n", p=P)).then_inc(weights_loaded, 16)
                sp.dma_start(w3[:], W3.rearrange("(c p) o -> p (c o)", p=P),
                             allow_slow_non_contiguous=True).then_inc(weights_loaded, 16)
                sp.dma_start(bias1[:], b1.rearrange("(c p) -> p c", p=P),
                             allow_slow_non_contiguous=True).then_inc(weights_loaded, 16)
                sp.dma_start(bias2[:], b2.rearrange("(c p) -> p c", p=P),
                             allow_slow_non_contiguous=True).then_inc(weights_loaded, 16)

            def load_ids(t0, t1, loaded):
                src = ids[t0 * P:t1 * P, :].rearrange("(t p) f -> p t f", p=P)
                sp.dma_start(ids_sb[:, t0:t1, :], src).then_inc(loaded, 16)

            load_ids(0, TILES, ids_loaded[0])
            load_ids_all(0, 0)
            for j in range(NS):
                if j >= RAWS:
                    sp.wait_ge(hi_ready, j - RAWS + 1)
                    sp.wait_ge(lo_ready, j - RAWS + 1)
                src = tables[SELECTED[j]].rearrange("(k c) d -> k c d", c=VC)
                sp.dma_start(table_raw[j % RAWS], src).then_inc(raw_loaded[j % RAWS], 16)
                if j == 1:
                    load_ids_all(0, 1)
                if j == RAWS - 1:
                    load_ids(TILES, B // P, ids_loaded[1])
                    for t in range(TILES):
                        load_dense(0, t)
                if j == NS - 2:
                    load_weights()
            def next_inputs(m):
                for h in range(2):
                    sp.wait_ge(hot_ready, (m - 1) * (2 * NS) + 2 * (ID_PARTS[h][-1] + 1))
                    load_ids_all(m, h)
                for t in range(TILES):
                    sp.wait_ge(x_filled, x_before(m - 1, x_end(m - 1, t)))
                    load_dense(m, t)

            with sp.Fori(1, NM - 1) as m:
                next_inputs(m)
            next_inputs(NM - 1)
            i, n = tail_at(NM - 1, Q_Y)
            sp.wait_ge(tail_moved[i], n + 1)
            sp.dma_start(out.rearrange("(m g s) o -> g m (s o)", m=NM, s=PER), y[:]).then_inc(stored, 16)
            sp.wait_ge(stored, 16)

        @block.gpsimd
        def _(pool):
            def gather(m, t):
                if isinstance(m, int) and m == 0:
                    pool.wait_ge(ids_loaded[0], 16)
                    ids_t = ids_sb[:, t, :]
                else:
                    pool.wait_ge(idx_ready, (m - 1) * TILES + (t + 1))
                    pool.sem_inc(gathers_begun, 1)
                    ids_t = idx[t]
                for g, features in enumerate(feature_groups[t]):
                    for f in features:
                        if f > 0:
                            gather_table(rows[t][:, gathered_features.index(f), :], f - 1, ids_t, gathered[t][g])

            def gather_table(dst, table, ids_t, done):
                pool.indirect_dma_start(
                    out=dst, out_offset=None, in_=tables[table],
                    in_offset=bass.IndirectOffsetOnAxis(ap=ids_t[:, table:table + 1], axis=0)).then_inc(done, 16)

            def gather_extra(t):
                for g, features in enumerate(extra_groups):
                    for f in features:
                        gather_table(extra_rows[t][:, extra_features.index(f), :], f - 1, idx[t], extra_gathered[t][g])

            pool.iota(row_i[:], pattern=[[1, VC]], base=0, channel_multiplier=VC).then_inc(iota_ready, 1)
            pool.memset(ident[:], 0.0).then_inc(ident_ready, 1)
            pool.wait_ge(ident_ready, 1)
            pool.affine_select(out=ident[:], in_=ident[:], compare_op=ALU.not_equal, fill=1.0, base=0,
                               pattern=[[-1, P]], channel_multiplier=1).then_inc(ident_ready, 1)
            for t in range(TILES):
                gather(0, t)
            with pool.Fori(1, NM - 1) as m:
                for t in range(TILES):
                    gather(m, t)
            gather(NM - 1, 0)
            pool.wait_ge(joined[1], NM - 1)
            pool.sem_inc(gathers_begun, 1)
            gather_extra(0)
            gather(NM - 1, 1)
            gather_extra(1)

        @block.tensor
        def _(pe):
            def x_bank(m, k):
                i = x_bank_of(m, k)
                wait(pe, x_moved[i], x_before(m, k, i))
                return x_ps[i]

            def transposes(m, t, g0, g1):
                for g in range(g0, g1):
                    features = groups(m, t)[g]
                    extra = g - len(feature_groups[t])
                    if extra < 0:
                        pe.wait_ge(gathered[t][g], (m + 1) * 16 * sum(f > 0 for f in features))
                    else:
                        pe.wait_ge(extra_gathered[t][extra], 16 * len(features))
                    if features[0] == 0:
                        pe.wait_ge(dense_loaded[t], (m + 1) * 16)
                    bank = x_bank(m, x_use(m, "rows", t, g))
                    for j, f in enumerate(features):
                        if extra < 0:
                            src = rows[t][:, gathered_features.index(f), :]
                        else:
                            src = extra_rows[t][:, extra_features.index(f), :]
                        last = pe.transpose(bank[:, j, :], src, ident[:])
                    last.then_inc(x_filled, 1)

            def select(m, j):
                if j >= num_selected(m + 1):
                    return
                first = isinstance(m, int) and m < 0
                if first:
                    pe.wait_ge(hi_ready, j + 1)
                bank = x_bank(m, x_use(m, "table", j))[:].rearrange("p a b -> p (a b)")[:, 0:MACRO]
                steps = [(c, part) for c in range(VC) for part in PARTS]
                if first:
                    steps.sort(key=lambda step: step[1])
                for n, (c, part) in enumerate(steps):
                    if c % HALF == 0 and part == "hi":
                        pe.wait_ge(hot_ready, (m + 1) * (2 * NS) + (2 * j + c // HALF + 1))
                    if first and n == VC:
                        pe.wait_ge(lo_ready, j + 1)
                    table = table_hi if part == "hi" else table_lo
                    last = pe.matmul(bank, table[j][:, c, :], hot[j % HOTS][:, c, :],
                                     start=(n == 0), stop=(n == len(steps) - 1))
                last.then_inc(x_filled, 1)

            def gram_products(m, t, u):
                if u == 0:
                    if isinstance(m, int) and m == 0:
                        pe.wait_ge(pads_ready, t + 1)
                    for i in range(2):
                        pe.wait_ge(x_moved[i], x_before(m, x_end(m, t), i))
                    pe.wait_ge(joined[t], m + 1)
                k = t * UNITS + u
                for e in range(2):
                    wait(pe, gram_moved[e], m * (TILES * UNITS) + (k - 1))
                for i in range(UNIT):
                    a = PER * (u * UNIT + i)
                    last = pe.matmul(
                        gram_ps[k % 2][:, i // PER_BANK, (i % PER_BANK) * SW:(i % PER_BANK + 1) * SW],
                        x[t][:, a:a + PER, :], x[t][:, a:a + PER, 0:F], start=True, stop=True)
                last.then_inc(gram_filled, 1)

            def tail_bank(m, q):
                i, n = tail_at(m, q)
                wait(pe, tail_moved[i], n)
                return tail_banks[i]

            def tail_ready(m, q):
                for earlier in range(max(0, q - (4 if is_last(m) else 2)), q):
                    wait_tail_moved(pe, m, earlier)

            def pair_transposes(m, q0, q1):
                if q0 == 0:
                    for e in range(2):
                        pe.wait_ge(gram_moved[e], (m + 1) * (TILES * UNITS))
                for q in range(q0, q1):
                    bank = tail_bank(m, q)
                    for j, f in enumerate(pair_banks[q]):
                        last = pe.transpose(bank[:, j * P:(j + 1) * P],
                                            gram[:, f:f + 2, :].rearrange("p f g -> p (f g)"), ident[:])
                    last.then_inc(tail_filled, 1)

            def chunk_transposes(m, c0, c1):
                for c in range(c0, c1):
                    tail_ready(m, sum(first_pair[fs[0]] < (c + 1) * KP for fs in pair_banks))
                    bank = tail_bank(m, Q_CHUNK + c)
                    pe.sem_inc(tail_begun, 1)
                    for s in range(PER):
                        last = pe.transpose(bank[0:KP, s * GROUPS:(s + 1) * GROUPS],
                                            pairs[:, s, c * KP:(c + 1) * KP], ident[0:GROUPS, 0:GROUPS])
                    last.then_inc(tail_filled, 1)

            def product(bank, operands):
                for n, (w, v, ready) in enumerate(operands):
                    ready()
                    for a, b in ((0, 0), (0, 1), (1, 0)):
                        last = pe.matmul(bank, w[a], v[b], start=(n == a == b == 0),
                                         stop=(n == len(operands) - 1 and a == 1))
                last.then_inc(tail_filled, 1)

            def layer1(m, n):
                def dense_ready():
                    pe.wait_ge(dense_kept, m + 1)

                def chunk_ready(c):
                    wait_tail_moved(pe, m, Q_CHUNK + c)

                bank = tail_bank(m, Q_H1 + n)[:, 0:MACRO]
                cols = slice(n * P, (n + 1) * P)
                operands = [([w[:, cols] for w in w1d], [v[:].rearrange("p s g -> p (s g)") for v in dense_t],
                             dense_ready)]
                operands += [([w[:, c, cols] for w in w1p], [pairs_t[:, i, c, :] for i in range(2)],
                              lambda c=c: chunk_ready(c)) for c in range(KC)]
                product(bank, operands)

            def layer2(m, n):
                def hidden_ready(c):
                    pe.wait_ge(h1_split, m * N1 + (c + 2))

                bank = tail_bank(m, Q_H2 + n)[:, 0:MACRO]
                cols = slice(n * P, (n + 1) * P)
                product(bank, [([w[:, c, cols] for w in w2], [h1[:, i, c, :] for i in range(2)],
                                lambda c=c: hidden_ready(c)) for c in range(N1)])

            def layer3(m):
                tail_ready(m, Q_Y)
                bank = tail_bank(m, Q_Y)
                for s in range(PER):
                    for c in range(N2):
                        last = pe.matmul(bank[0:GROUPS, s:s + 1], h2[:, c, s * GROUPS:(s + 1) * GROUPS],
                                         w3[:, c:c + 1], start=(c == 0), stop=(c == N2 - 1))
                last.then_inc(tail_filled, 1)

            def macro_tile(m, before, ahead):
                transposes(m, 0, EARLY, 3)
                if before:
                    pair_transposes(m - 1, 0, 1)
                transposes(m, 0, 3, 4)
                if before:
                    pair_transposes(m - 1, 1, 2)
                if ahead:
                    select(m, 0)
                if before:
                    pair_transposes(m - 1, 2, Q_CHUNK)
                transposes(m, 0, 4, len(groups(m, 0)))
                if ahead:
                    select(m, 1)
                if before:
                    chunk_transposes(m - 1, 0, 2)
                if ahead:
                    select(m, 2)
                gram_products(m, 0, 0)
                if before:
                    chunk_transposes(m - 1, 2, KC)
                for u in range(1, UNITS):
                    transposes(m, 1, u - 1, u)
                    gram_products(m, 0, u)
                    if before:
                        layer1(m - 1, u - 1)
                transposes(m, 1, 3, 4)
                if ahead:
                    select(m, 3)
                if before:
                    layer1(m - 1, 3)
                transposes(m, 1, 4, 5)
                if ahead:
                    select(m, 4)
                transposes(m, 1, 5, len(feature_groups[1]))
                if before:
                    layer2(m - 1, 0)
                transposes(m, 1, len(feature_groups[1]), len(groups(m, 1)))
                if is_last(m):
                    layer2(m - 1, 1)
                gram_products(m, 1, 0)
                if before and not is_last(m):
                    layer2(m - 1, 1)
                gram_products(m, 1, 1)
                if ahead:
                    select(m, 5)
                if before:
                    layer3(m - 1)
                if ahead:
                    select(m, 6)
                gram_products(m, 1, 2)
                if ahead:
                    select(m, 7)
                if not is_last(m):
                    transposes(m + 1, 0, 0, 1)
                gram_products(m, 1, 3)
                if not is_last(m):
                    transposes(m + 1, 0, 1, EARLY)

            for j in range(NS):
                select(-1, j)
            pe.wait_ge(ident_ready, 2)
            transposes(0, 0, 0, EARLY)
            macro_tile(0, False, True)
            pe.wait_ge(w_lo_ready, 3)
            with pe.Fori(1, NM - 2) as m:
                macro_tile(m, True, True)
            macro_tile(NM - 2, True, True)
            macro_tile(NM - 1, True, False)
            pair_transposes(NM - 1, 0, Q_CHUNK)
            chunk_transposes(NM - 1, 0, KC)
            for n in range(N1):
                layer1(NM - 1, n)
            for n in range(N2):
                layer2(NM - 1, n)
            layer3(NM - 1)

        def gram_quadrants(copy, e, k):
            for s in (2 * e, 2 * e + 1):
                rows_s = slice(QUAD * s, QUAD * (s + 1))
                src = gram_ps[k % 2][rows_s, :, 0:PER_BANK * SW]
                src = src.rearrange("p b (i s f) -> p b i s f", s=PER, f=F)[:, :, :, s, :]
                dst = gram[rows_s, :, k * UNIT:(k + 1) * UNIT]
                last = copy(dst.rearrange("p f (b i) -> p b i f", b=UNIT_BANKS), src)
            return last

        def pair_columns(copy, m, q):
            for j, f0 in enumerate(pair_banks[q]):
                for i in range(2):
                    f = f0 + i
                    block_f = tail_banks[tail_at(m, q)[0]][i * GROUPS:(i + 1) * GROUPS, j * P:(j + 1) * P]
                    n = F - 1 - f
                    last = copy(pairs[:, :, first_pair[f]:first_pair[f] + n],
                                block_f.rearrange("p (s f) -> p s f", f=QUAD)[:, :, f + 1:F])
            return last

        @block.scalar
        def _(act):
            def copy(dst, src):
                return act.activation(dst, src, ACT.Copy)

            def transposes(m, t, g0, g1):
                for g in range(g0, g1):
                    features = groups(m, t)[g]
                    k = x_use(m, "rows", t, g)
                    bank = x_bank_of(m, k)
                    act.wait_ge(x_filled, x_before(m, k + 1))
                    if g == 0:
                        wait(act, dense_kept, m)
                        copy(dense_new[:, :, t * QUAD:(t + 1) * QUAD],
                             x_ps[bank][:, 0, :].rearrange("p (g s) -> p s g", s=PER))
                    for i, f, step, n in runs(features):
                        last = copy(x[t][:, :, f:f + (n - 1) * step + 1:step],
                                    x_ps[bank][:, i:i + n, :].rearrange("p f b -> p b f"))
                    last.then_inc(x_moved[bank], 1)
                    if g == len(feature_groups[t]) - 1 and not is_last(m):
                        index(m + 1, t)

            def index(m, t):
                copy(idx[t][:], ids_sb[:, m * TILES + t, :]).then_inc(idx_ready, 1)

            def select(m, j):
                if j >= num_selected(m + 1):
                    return
                if not (isinstance(m, int) and m < 0):
                    act.wait_ge(joined[1], m + 1)
                k = x_use(m, "table", j)
                bank = x_bank_of(m, k)
                act.wait_ge(x_filled, x_before(m, k + 1))
                src = x_ps[bank][:].rearrange("p a b -> p (a b)")[:, 0:MACRO]
                copy(picked[:, j, :], src).then_inc(x_moved[bank], 1)

            def join(m, t):
                wait(act, gram_filled, (m - 1) * (TILES * UNITS) + (t + 1) * UNITS)
                for i in range(2):
                    act.wait_ge(x_moved[i], x_before(m, -EARLY, i))
                for i, f, step, n in runs(selected_features[:num_selected(m)]):
                    last = copy(x[t][:, :, f:f + (n - 1) * step + 1:step],
                                picked[:, i:i + n, t * P:(t + 1) * P].rearrange("p f b -> p b f"))
                last.then_inc(joined[t], 1)

            def keep_dense(m):
                for t in range(TILES):
                    k = x_use(m, "rows", t, 0)
                    act.wait_ge(x_moved[x_bank_of(m, k)], x_before(m, k + 1, x_bank_of(m, k)))
                copy(dense_t[0][:], dense_new[:]).then_inc(dense_hi_kept, 1)

            def gram_products(m, t, u):
                k = t * UNITS + u
                act.wait_ge(gram_filled, m * (TILES * UNITS) + (k + 1))
                gram_quadrants(copy, 0, k).then_inc(gram_moved[0], 1)

            def pair_transposes(m, q):
                act.wait_ge(tail_filled, m * T_USES + (q + 1))
                pair_columns(copy, m, q).then_inc(tail_moved[tail_at(m, q)[0]], 1)

            def chunk_transposes(m, c0, c1):
                for c in range(c0, c1):
                    q = Q_CHUNK + c
                    act.wait_ge(tail_filled, m * T_USES + (q + 1))
                    copy(pairs_t[:, 0, c, :], tail_banks[tail_at(m, q)[0]][0:KP, 0:MACRO]).then_inc(pairs_hi_moved, 1)

            def layer1(m, n):
                q = Q_H1 + n
                act.wait_ge(tail_filled, m * T_USES + (q + 1))
                act.wait_ge(h1_split, m * N1 + n)
                bank = tail_at(m, q)[0]
                src = tail_banks[bank][:, 0:MACRO]
                act.activation(h1_new[:, n % 2, :], src, ACT.Relu, bias=bias1[:, n:n + 1]).then_inc(h1_moved, 1)
                act.activation(h1[:, 0, n, :], src, ACT.Relu, bias=bias1[:, n:n + 1]).then_inc(tail_moved[bank], 1)

            def layer2(m, n):
                q = Q_H2 + n
                act.wait_ge(tail_filled, m * T_USES + (q + 1))
                bank = tail_at(m, q)[0]
                act.activation(h2[:, n, :], tail_banks[bank][:, 0:MACRO], ACT.Relu,
                               bias=bias2[:, n:n + 1]).then_inc(tail_moved[bank], 1)

            def layer3(m):
                act.wait_ge(tail_filled, m * T_USES + (Q_Y + 1))
                bank = tail_at(m, Q_Y)[0]
                copy(y[:, m, :], tail_banks[bank][0:GROUPS, 0:PER]).then_inc(tail_moved[bank], 1)

            def macro_tile(m, before, ahead):
                transposes(m, 0, EARLY, 3)
                if before:
                    pair_transposes(m - 1, 0)
                transposes(m, 0, 3, 4)
                if not before:
                    act.wait_ge(lo_ready, NS)
                join(m, 1)
                if ahead:
                    select(m, 0)
                if before:
                    pair_transposes(m - 1, 2)
                transposes(m, 0, 4, len(groups(m, 0)))
                if ahead:
                    select(m, 1)
                if before:
                    chunk_transposes(m - 1, 0, 2)
                if ahead:
                    select(m, 2)
                if not before:
                    act.wait_ge(w_lo_ready, 1)
                gram_products(m, 0, 0)
                if before:
                    chunk_transposes(m - 1, 2, KC)
                for u in range(1, UNITS):
                    transposes(m, 1, u - 1, u)
                    gram_products(m, 0, u)
                    if before:
                        layer1(m - 1, u - 1)
                transposes(m, 1, 3, 4)
                if ahead:
                    select(m, 3)
                if before:
                    layer1(m - 1, 3)
                else:
                    copy(w1p[0][:], w1p_raw[:]).then_inc(w_hi_ready[0], 1)
                transposes(m, 1, 4, 5)
                if ahead:
                    select(m, 4)
                transposes(m, 1, 5, len(feature_groups[1]))
                if before:
                    layer2(m - 1, 0)
                transposes(m, 1, len(feature_groups[1]), len(groups(m, 1)))
                if is_last(m):
                    layer2(m - 1, 1)
                gram_products(m, 1, 0)
                keep_dense(m)
                if before and not is_last(m):
                    layer2(m - 1, 1)
                gram_products(m, 1, 1)
                if ahead:
                    select(m, 5)
                if before:
                    layer3(m - 1)
                if ahead:
                    select(m, 6)
                gram_products(m, 1, 2)
                if ahead:
                    select(m, 7)
                    join(m + 1, 0)
                if not is_last(m):
                    transposes(m + 1, 0, 0, 1)
                gram_products(m, 1, 3)
                if not is_last(m):
                    transposes(m + 1, 0, 1, EARLY)

            act.nop().then_inc(tail_moved[0], 1)
            for j in range(NS):
                act.wait_ge(raw_loaded[j % RAWS], 16 * (j // RAWS + 1))
                copy(table_hi[j][:], table_raw[j % RAWS]).then_inc(hi_ready, 1)
                if j > 0:
                    select(-1, j - 1)
            act.wait_ge(weights_loaded, 16 * 7)
            copy(w2[0][:], w2_raw).then_inc(w_hi_ready[0], 1)
            select(-1, NS - 1)
            act.wait_ge(ids_loaded[1], 16)
            join(0, 0)
            transposes(0, 0, 0, EARLY)
            macro_tile(0, False, True)
            act.wait_ge(w_lo_ready, 3)
            with act.Fori(1, NM - 2) as m:
                macro_tile(m, True, True)
            macro_tile(NM - 2, True, True)
            macro_tile(NM - 1, True, False)
            for q in range(0, Q_CHUNK, 2):
                pair_transposes(NM - 1, q)
            chunk_transposes(NM - 1, 0, KC)
            for n in range(N1):
                layer1(NM - 1, n)
            for n in range(N2):
                layer2(NM - 1, n)
            layer3(NM - 1)

        @block.vector
        def _(dve):
            def copy(dst, src):
                return dve.tensor_copy(dst, src)

            def low_part(lo, whole, hi):
                return dve.tensor_tensor(lo, whole, hi.bitcast(F32), ALU.subtract)

            def selected(m, j):
                if isinstance(m, int) and m == 0:
                    return j + 1
                return x_before(m - 1, x_use(m - 1, "table", j) + 1)

            def build_hot(m, j, c0=0, c1=VC):
                if j >= num_selected(m):
                    return
                if c0 == 0:
                    dve.wait_ge(ids_all_loaded[0 if j in ID_PARTS[0] else 1], (m + 1) * 16)
                    if j >= HOTS:
                        dve.wait_ge(x_filled, selected(m, j - HOTS))
                    elif not (isinstance(m, int) and m == 0):
                        dve.wait_ge(x_filled, selected(m - 1, NS - 1 - (NS - 1 - j) % HOTS))
                for c in range(c0, c1):
                    last = dve.tensor_scalar(hot[j % HOTS][:, c, :], ids_all[0:VK, j, :],
                                             row_f[0:VK, c:c + 1], None, ALU.is_equal)
                    if c % HALF == HALF - 1:
                        last.then_inc(hot_ready, 1)

            def keep_dense(m):
                dve.wait_ge(dense_hi_kept, m + 1)
                low_part(dense_t[1][:], dense_new[:], dense_t[0][:]).then_inc(dense_kept, 1)

            def gram_products(m, k):
                dve.wait_ge(gram_filled, m * (TILES * UNITS) + (k + 1))
                gram_quadrants(copy, 1, k).then_inc(gram_moved[1], 1)

            def pair_transposes(m, q):
                dve.wait_ge(tail_filled, m * T_USES + (q + 1))
                pair_columns(copy, m, q).then_inc(tail_moved[tail_at(m, q)[0]], 1)

            def chunk_transposes(m, c0, c1):
                for c in range(c0, c1):
                    q = Q_CHUNK + c
                    dve.wait_ge(pairs_hi_moved, m * KC + (c + 1))
                    bank = tail_at(m, q)[0]
                    low_part(pairs_t[:, 1, c, :], tail_banks[bank][0:KP, 0:MACRO],
                             pairs_t[:, 0, c, :]).then_inc(tail_moved[bank], 1)

            def layer1(m, n):
                dve.wait_ge(h1_moved, m * N1 + (n + 1))
                wait_tail_moved(dve, m, Q_H1 + n)
                low_part(h1[:, 1, n, :], h1_new[:, n % 2, :], h1[:, 0, n, :]).then_inc(h1_split, 1)

            def macro_tile(m, before, ahead):
                hots = build_hot if ahead else lambda *a: None
                hots(m + 1, 0, 0, HALF)
                if before:
                    gram_products(m - 1, TILES * UNITS - 1)
                hots(m + 1, 0, HALF, VC)
                hots(m + 1, 1, 0, HALF)
                if before:
                    pair_transposes(m - 1, 1)
                hots(m + 1, 1, HALF, VC)
                if before:
                    pair_transposes(m - 1, 3)
                hots(m + 1, 2)
                if before:
                    chunk_transposes(m - 1, 0, 2)
                else:
                    split_layer2()
                gram_products(m, 0)
                if before:
                    chunk_transposes(m - 1, 2, KC)
                gram_products(m, 1)
                if before:
                    layer1(m - 1, 0)
                hots(m + 1, 3, 0, HALF)
                gram_products(m, 2)
                if before:
                    layer1(m - 1, 1)
                hots(m + 1, 3, HALF, VC)
                gram_products(m, 3)
                if before:
                    layer1(m - 1, 2)
                hots(m + 1, 4)
                if before:
                    layer1(m - 1, 3)
                else:
                    split_layer1()
                hots(m + 1, 5, 0, HALF)
                gram_products(m, UNITS)
                keep_dense(m)
                hots(m + 1, 5, HALF, VC)
                gram_products(m, UNITS + 1)
                hots(m + 1, 6)
                hots(m + 1, 7)
                gram_products(m, UNITS + 2)

            def split_layer2():
                dve.wait_ge(w_hi_ready[0], 1)
                low_part(w2[1][:], w2_raw, w2[0][:]).then_inc(w_lo_ready, 1)
                dve.wait_ge(w_lo_ready, 1)

            def split_layer1():
                dve.wait_ge(lo_ready, NS)
                dve.memset(x[1][:, :, F:QUAD], 0.0).then_inc(pads_ready, 1)
                dve.tensor_tensor(w1a_raw, w1a_raw, w1b_raw, ALU.add).then_inc(w_summed, 1)
                dve.wait_ge(w_summed, 1)
                copy(w1d[0][:], w1a_raw).then_inc(w_hi_ready[1], 1)
                dve.wait_ge(w_hi_ready[0], 2)
                low_part(w1p[1][:], w1p_raw[:], w1p[0][:]).then_inc(w_lo_ready, 1)
                dve.wait_ge(w_hi_ready[1], 1)
                low_part(w1d[1][:], w1a_raw, w1d[0][:]).then_inc(w_lo_ready, 1)

            dve.nop().then_inc(tail_moved[1], 1)
            dve.nop().then_inc(h1_split, 1)
            dve.memset(x[0][:, :, F:QUAD], 0.0).then_inc(pads_ready, 1)
            dve.wait_ge(iota_ready, 1)
            copy(row_f[:], row_i[:]).then_inc(rows_ready, 1)
            dve.wait_ge(rows_ready, 1)
            def split_table(j):
                dve.wait_ge(hi_ready, j + 1)
                low_part(table_lo[j][:], table_raw[j % RAWS], table_hi[j][:]).then_inc(lo_ready, 1)

            for j in range(HOTS):
                build_hot(0, j)
            for j in range(HOTS):
                split_table(j)
            for j in range(HOTS, NS):
                build_hot(0, j)
                split_table(j)
            macro_tile(0, False, True)
            with dve.Fori(1, NM - 2) as m:
                macro_tile(m, True, True)
            macro_tile(NM - 2, True, True)
            macro_tile(NM - 1, True, False)
            gram_products(NM - 1, TILES * UNITS - 1)
            for q in range(1, Q_CHUNK, 2):
                pair_transposes(NM - 1, q)
            chunk_transposes(NM - 1, 0, KC)
            for n in range(N1):
                layer1(NM - 1, n)


_INS = (["r_dense_features", "ids"] + [f"tbl_{f}" for f in range(NUM_TABLES)]
        + ["W_top1", "b_top1", "W_top2", "b_top2", "W_top3"])


def kernel(**inputs):
    import numpy as _np
    import concourse.bacc as _bacc
    from concourse import mybir as _mybir
    from concourse.bass_utils import run_bass_kernel_spmd as _run

    nc = _bacc.Bacc("TRN2", target_bir_lowering=False, num_devices=1)
    given = {name: _np.ascontiguousarray(inputs[name]) for name in _INS}
    given["selected_ids"] = _np.ascontiguousarray(given["ids"].T[SELECTED])
    arrays, aps = {}, {}
    for name, a in given.items():
        arrays[f"in_{name}_dram"] = a
        aps[name] = nc.dram_tensor(f"in_{name}_dram", a.shape, _mybir.dt.from_np(a.dtype), kind="ExternalInput").ap()
    batch = inputs["r_dense_features"].shape[0]
    out = nc.dram_tensor("out_0_dram", (batch, 1), _mybir.dt.float32, kind="ExternalOutput").ap()
    dlrm_kernel(nc, aps["r_dense_features"], aps["ids"], aps["selected_ids"],
                [aps[f"tbl_{f}"] for f in range(NUM_TABLES)],
                aps["W_top1"], aps["b_top1"], aps["W_top2"], aps["b_top2"], aps["W_top3"], out)
    r = _run(nc, [arrays], core_ids=[0])
    return r.results[0]["out_0_dram"]
```
